# Optimizing a Trainium2 kernel written in Bass

```python
import numpy as np
import jax
import jax.numpy as jnp

def _softmax(x, axis=-1):
    return jax.nn.softmax(x, axis=axis)

def _gelu(x):
    return jax.nn.gelu(x, approximate=True)

def _silu(x):
    return jax.nn.silu(x)

def _sigmoid(x):
    return jax.nn.sigmoid(x)

def _layernorm(x, axis=-1, eps=1e-05):
    m = jnp.mean(x, axis=axis, keepdims=True)
    v = jnp.var(x, axis=axis, keepdims=True)
    return (x - m) / jnp.sqrt(v + eps)

def _scatter_add(tgt, idx, src, axis=0):
    return tgt.at[idx].add(src)

def _segment_sum(src, seg, n):
    return jax.ops.segment_sum(src, seg, n)
kernel_name = 'mk_xattn_ffn_d1_seqx_r8_5ba744'

def setup_inputs(seed: int=0):
    np.random.seed(seed)
    _w = jnp.asarray

    def _rec_inputs():
        import jax
        import jax.numpy as jnp
        _rk = jax.random.key(seed)
        x = -7.109e-05 + 0.9999 * jax.random.normal(jax.random.fold_in(_rk, 1), (16, 256, 128), jnp.float32)
        _lenS = 256 - jax.random.randint(jax.random.fold_in(_rk, 7), (16,), 0, max(1, 256 // 4) + 1, jnp.int32)
        _lenS2 = 1601 - jax.random.randint(jax.random.fold_in(_rk, 8), (16,), 0, max(1, 1601 // 4) + 1, jnp.int32)
        _ctx_768P = jax.random.normal(jax.random.fold_in(_rk, 11), (16, 16, 96), jnp.float32)
        _ctx_768c = jax.random.dirichlet(jax.random.fold_in(_rk, 511), 0.3 * jnp.ones((16,), jnp.float32), (16, 1601))
        _ctx_768t = jnp.einsum('bsk,bkd->bsd', _ctx_768c, _ctx_768P)
        _ctx_768t = _ctx_768t * jax.lax.rsqrt(jnp.mean(jnp.square(_ctx_768t)) + 1e-12) * 0.953939
        ctx_768 = 0.000486113 + 1.00014 * (_ctx_768t + 0.3 * jax.random.normal(jax.random.fold_in(_rk, 611), (16, 1601, 96), jnp.float32))
        return (x, ctx_768)
    x, ctx_768 = _rec_inputs()

    def _L0_xattn_setup():
        import jax, jax.numpy as jnp
        import numpy as np
        HEADS = 16
        DIM_HEAD = 64
        SCALE = DIM_HEAD ** (-0.5)
        key = jax.random.key(seed)
        ks = jax.random.split(key, 7)
        B, Nq, Dq = (16, 512, 128)
        Nc, Dc = (77, 96)
        inner = HEADS * DIM_HEAD
        return {'x': jax.random.normal(ks[0], (B, Nq, Dq), jnp.float32), 'context': jax.random.normal(ks[1], (B, Nc, Dc), jnp.float32), 'Wq': jax.random.normal(ks[2], (Dq, inner), jnp.float32) * Dq ** (-0.5), 'Wk': jax.random.normal(ks[3], (Dc, inner), jnp.float32) * Dc ** (-0.5), 'Wv': jax.random.normal(ks[4], (Dc, inner), jnp.float32) * Dc ** (-0.5), 'Wo': jax.random.normal(ks[5], (inner, Dq), jnp.float32) * inner ** (-0.5), 'bo': jnp.zeros((Dq,), jnp.float32)}
    _L0_xattn_all = _L0_xattn_setup()
    _L0_xattn_in = {k: v for k, v in _L0_xattn_all.items() if k in ('Wq', 'Wk', 'Wv', 'Wo', 'bo')}
    del _L0_xattn_all

    def _L0_ffn_setup():
        import jax, jax.numpy as jnp
        import numpy as np
        from jax import lax
        B, S, H = (2, 128, 128)
        I = 64
        E = 32
        TOP_K = 4
        N_GROUP = 4
        TOPK_GROUP = 2
        SCALE = 2.5
        N_SHARED = 2
        SH_I = I * N_SHARED

        def _route(tokens, router_weight, router_bias):
            logits = tokens.astype(jnp.float32) @ router_weight.astype(jnp.float32).T
            scores = jax.nn.sigmoid(logits)
            sfc = scores + router_bias[None, :]
            T = tokens.shape[0]
            grp = sfc.reshape(T, N_GROUP, E // N_GROUP)
            group_scores = lax.top_k(grp, 2)[0].sum(-1)
            _, gidx = lax.top_k(group_scores, TOPK_GROUP)
            gmask = jax.nn.one_hot(gidx, N_GROUP, dtype=sfc.dtype).sum(1)
            smask = jnp.broadcast_to(gmask[:, :, None], (T, N_GROUP, E // N_GROUP)).reshape(T, E)
            tmp = jnp.where(smask > 0, sfc, 0.0)
            _, topk_idx = lax.top_k(tmp, TOP_K)
            topk_w = jnp.take_along_axis(scores, topk_idx, axis=1)
            topk_w = topk_w / (topk_w.sum(-1, keepdims=True) + 1e-20)
            topk_w = topk_w * SCALE
            return (topk_idx, topk_w)
        key = jax.random.key(seed)
        ks = jax.random.split(key, 10)
        std = 0.02
        return {'hidden_states': jax.random.normal(ks[0], (B, S, H), jnp.float32), 'router_weight': jax.random.normal(ks[1], (E, H), jnp.float32) * std, 'router_bias': jnp.zeros((E,), jnp.float32), 'gate_w': jax.random.normal(ks[2], (E, I, H), jnp.float32) * std, 'up_w': jax.random.normal(ks[3], (E, I, H), jnp.float32) * std, 'down_w': jax.random.normal(ks[4], (E, H, I), jnp.float32) * std, 'shared_gate_w': jax.random.normal(ks[5], (SH_I, H), jnp.float32) * std, 'shared_up_w': jax.random.normal(ks[6], (SH_I, H), jnp.float32) * std, 'shared_down_w': jax.random.normal(ks[7], (H, SH_I), jnp.float32) * std}
    _L0_ffn_all = _L0_ffn_setup()
    _L0_ffn_in = {k: v for k, v in _L0_ffn_all.items() if k in ('router_weight', 'router_bias', 'gate_w', 'up_w', 'down_w', 'shared_gate_w', 'shared_up_w', 'shared_down_w')}
    del _L0_ffn_all
    return {'x': x, 'ctx_768': ctx_768, 'L0_xattn_Wq': _L0_xattn_in['Wq'], 'L0_xattn_Wk': _L0_xattn_in['Wk'], 'L0_xattn_Wv': _L0_xattn_in['Wv'], 'L0_xattn_Wo': _L0_xattn_in['Wo'], 'L0_xattn_bo': _L0_xattn_in['bo'], 'L0_ffn_router_weight': _L0_ffn_in['router_weight'], 'L0_ffn_router_bias': _L0_ffn_in['router_bias'], 'L0_ffn_gate_w': _L0_ffn_in['gate_w'], 'L0_ffn_up_w': _L0_ffn_in['up_w'], 'L0_ffn_down_w': _L0_ffn_in['down_w'], 'L0_ffn_shared_gate_w': _L0_ffn_in['shared_gate_w'], 'L0_ffn_shared_up_w': _L0_ffn_in['shared_up_w'], 'L0_ffn_shared_down_w': _L0_ffn_in['shared_down_w']}

def reference(x, ctx_768, L0_xattn_Wq, L0_xattn_Wk, L0_xattn_Wv, L0_xattn_Wo, L0_xattn_bo, L0_ffn_router_weight, L0_ffn_router_bias, L0_ffn_gate_w, L0_ffn_up_w, L0_ffn_down_w, L0_ffn_shared_gate_w, L0_ffn_shared_up_w, L0_ffn_shared_down_w):
    import jax
    import jax.numpy as jnp

    def _L0_xattn_ref(x, context, Wq, Wk, Wv, Wo, bo):
        import jax, jax.numpy as jnp
        import numpy as np
        HEADS = 16
        DIM_HEAD = 64
        SCALE = DIM_HEAD ** (-0.5)
        B, Nq, _ = x.shape
        Nc = context.shape[1]
        q = (x @ Wq).reshape(B, Nq, HEADS, DIM_HEAD).transpose(0, 2, 1, 3)
        k = (context @ Wk).reshape(B, Nc, HEADS, DIM_HEAD).transpose(0, 2, 1, 3)
        v = (context @ Wv).reshape(B, Nc, HEADS, DIM_HEAD).transpose(0, 2, 1, 3)
        sim = jnp.einsum('bhid,bhjd->bhij', q, k) * SCALE
        attn = jax.nn.softmax(sim, axis=-1)
        out = jnp.einsum('bhij,bhjd->bhid', attn, v)
        out = out.transpose(0, 2, 1, 3).reshape(B, Nq, HEADS * DIM_HEAD)
        return out @ Wo + bo

    def _L0_ffn_ref(hidden_states, router_weight, router_bias, gate_w, up_w, down_w, shared_gate_w, shared_up_w, shared_down_w):
        import jax, jax.numpy as jnp
        import numpy as np
        from jax import lax
        B, S, H = (2, 128, 128)
        I = 64
        E = 32
        TOP_K = 4
        N_GROUP = 4
        TOPK_GROUP = 2
        SCALE = 2.5
        N_SHARED = 2
        SH_I = I * N_SHARED

        def _route(tokens, router_weight, router_bias):
            logits = tokens.astype(jnp.float32) @ router_weight.astype(jnp.float32).T
            scores = jax.nn.sigmoid(logits)
            sfc = scores + router_bias[None, :]
            T = tokens.shape[0]
            grp = sfc.reshape(T, N_GROUP, E // N_GROUP)
            group_scores = lax.top_k(grp, 2)[0].sum(-1)
            _, gidx = lax.top_k(group_scores, TOPK_GROUP)
            gmask = jax.nn.one_hot(gidx, N_GROUP, dtype=sfc.dtype).sum(1)
            smask = jnp.broadcast_to(gmask[:, :, None], (T, N_GROUP, E // N_GROUP)).reshape(T, E)
            tmp = jnp.where(smask > 0, sfc, 0.0)
            _, topk_idx = lax.top_k(tmp, TOP_K)
            topk_w = jnp.take_along_axis(scores, topk_idx, axis=1)
            topk_w = topk_w / (topk_w.sum(-1, keepdims=True) + 1e-20)
            topk_w = topk_w * SCALE
            return (topk_idx, topk_w)
        tokens = hidden_states.reshape(-1, H)
        topk_idx, topk_w = _route(tokens, router_weight, router_bias)
        gate_vals = jax.nn.silu(jnp.einsum('th,eih->tei', tokens, gate_w))
        up_vals = jnp.einsum('th,eih->tei', tokens, up_w)
        hidden_vals = gate_vals * up_vals
        expert_out = jnp.einsum('tei,ehi->teh', hidden_vals, down_w)
        sel = jnp.take_along_axis(expert_out, topk_idx[:, :, None], axis=1)
        mixed = (sel * topk_w[:, :, None].astype(sel.dtype)).sum(1)
        mixed = mixed.reshape(hidden_states.shape)
        sg = jax.nn.silu(jnp.einsum('bsh,ih->bsi', hidden_states, shared_gate_w))
        su = jnp.einsum('bsh,ih->bsi', hidden_states, shared_up_w)
        shared = jnp.einsum('bsi,hi->bsh', sg * su, shared_down_w)
        return mixed + shared
    x = x + _L0_xattn_ref(_layernorm(x, axis=-1), ctx_768, L0_xattn_Wq, L0_xattn_Wk, L0_xattn_Wv, L0_xattn_Wo, L0_xattn_bo)
    x = x + _L0_ffn_ref(_layernorm(x, axis=-1), L0_ffn_router_weight, L0_ffn_router_bias, L0_ffn_gate_w, L0_ffn_up_w, L0_ffn_down_w, L0_ffn_shared_gate_w, L0_ffn_shared_up_w, L0_ffn_shared_down_w)
    return x

_drawn_inputs = setup_inputs


def setup_inputs(seed=0):
    import zlib

    import numpy as np

    out = dict(_drawn_inputs(seed))
    spreads = {'L0_xattn_bo': (0.0, 0.1), 'L0_ffn_router_bias': (0.0, 0.8)}
    factors = {'L0_ffn_router_weight': 8.0,
     'L0_ffn_gate_w': 8.0,
     'L0_ffn_up_w': 8.0,
     'L0_ffn_down_w': 8.0,
     'L0_ffn_shared_gate_w': 8.0,
     'L0_ffn_shared_up_w': 8.0,
     'L0_ffn_shared_down_w': 8.0}
    for name, (base, spread) in spreads.items():
        noise = np.random.default_rng([zlib.crc32(name.encode()), seed]).standard_normal(out[name].shape)
        drawn = base * np.exp(spread * noise) if base else spread * noise
        out[name] = jnp.asarray(drawn.astype(out[name].dtype))
    for name, factor in factors.items():
        out[name] = (out[name] * factor).astype(out[name].dtype)
    return out
```

```python
from contextlib import ExitStack

import concourse.bass as bass
from concourse import mybir

ALU = mybir.AluOpType
ACT = mybir.ActivationFunctionType
AX = mybir.AxisListType
F32 = mybir.dt.float32
F32R = mybir.dt.float32r
I32 = mybir.dt.int32

P = 128
BANK = 512
TOP_K, N_EGROUP, TOPK_EGROUP, ROUTE_SCALE = 4, 4, 2, 2.5
EPS = 1e-5
BIG = 1e30


def xattn_moe(nc, x, ctx, Wq, Wk, Wv, Wo, bo, router_w, router_b, gate_w, up_w, down_w,
              sh_gate_w, sh_up_w, sh_down_w, out):
    B, NQ, D = x.shape
    _, NC, DC = ctx.shape
    INNER = Wq.shape[1]
    DH = 64
    H = INNER // DH
    E, EI, _ = gate_w.shape
    SCALE = float(DH) ** -0.5
    assert D == P and NQ == 2 * P and H == 16 and EI * 2 == P and sh_gate_w.shape[0] == P

    GH = 4
    GQ = GH * NQ
    NGB = H // GH
    NG = B * NGB
    FULL = NC // P
    TAIL = NC - FULL * P
    S = FULL + 1
    QT = 4
    SPAD = NGB * QT
    MAXW = 402
    NKPAD = 4 * MAXW
    DOUBLES = NKPAD - NC
    NM = 2 * (GQ // P)
    T = B * NQ // P
    NCH = T // 4
    NP = E // 2 + 1
    YW = D + 1
    OW = DC + 1

    stack = ExitStack()
    with stack:
        def sb(where, name, shape, dt=F32):
            return where.enter_context(nc.sbuf_tensor(name, shape, dt))

        def sem(name):
            return stack.enter_context(nc.semaphore(name))

        x1 = sb(stack, "x1", [P, T + 2, D])
        ident = sb(stack, "ident", [P, P])
        bo_rows = sb(stack, "bo_rows", [P, D])
        stats = sb(stack, "stats", [P, T, 6])
        mean = sb(stack, "mean", [P, T])
        dif = sb(stack, "dif", [P, T])
        var = sb(stack, "var", [P, T])
        std = sb(stack, "std", [P, T])
        rstd = sb(stack, "rstd", [P, T])
        xn = sb(stack, "xn", [P, 2, 4, D])
        recip = sb(stack, "recip", [P, 4])

        att = ExitStack()
        xnT = sb(att, "xnT", [P, (B + 1) * NQ])
        A_all = sb(att, "A_all", [P, H, DC])
        B_all = sb(att, "B_all", [OW, H, YW])
        A_stage = sb(att, "A_stage", [P, GH, DC])
        nat = sb(att, "nat", [P, 2, SPAD, DC])
        c_stage = sb(att, "c_stage", [P, QT, DC])
        cT_hi = sb(att, "cT_hi", [OW, 2, SPAD * P], F32R)
        cT_lo = sb(att, "cT_lo", [DC, 2, SPAD * P], F32R)
        v_hi = sb(att, "v_hi", [P, 2, SPAD, OW], F32R)
        v_lo = sb(att, "v_lo", [P, 2, SPAD, OW], F32R)
        qT_hi = sb(att, "qT_hi", [OW, 2, GQ], F32R)
        qT_lo = sb(att, "qT_lo", [DC, 2, GQ], F32R)
        qT_max = sb(att, "qT_max", [DC, GQ], F32R)
        m_part = sb(att, "m_part", [P, NM])
        m_neg = sb(att, "m_neg", [P, NM // 2])
        m_row = sb(att, "m_row", [NM // 2, P], F32R)
        oT = sb(att, "oT", [OW, GQ])
        with ExitStack() as early:
            Wq_sb = sb(early, "Wq_sb", [P, INNER])
            Wk_sb = sb(early, "Wk_sb", [DC, INNER])
            Wv_sb = sb(early, "Wv_sb", [DC, INNER])
            Wo_sb = sb(early, "Wo_sb", [P, INNER // P, D])
            WT = sb(early, "WT", [P, 3, P])
        p_full = sb(att, "p_full", [P, 2, GQ])
        p_hi = sb(att, "p_hi", [P, 4, GQ], F32R)
        p_lo = sb(att, "p_lo", [P, 4, GQ], F32R)
        att.close()

        moe = stack.enter_context(ExitStack())
        x2T_hi = sb(moe, "x2T_hi", [P, T * P], F32R)
        x2T_lo = sb(moe, "x2T_lo", [P, T * P], F32R)
        x2T_f = sb(moe, "x2T_f", [P, 2, BANK])
        w_nat = sb(moe, "w_nat", [P, 3, NP, P])
        gu_hi = sb(moe, "gu_hi", [P, 2, NP, P], F32R)
        gu_lo = sb(moe, "gu_lo", [P, 2, NP, P], F32R)
        dT = sb(moe, "dT", [P, NP, P])
        rw_nat = sb(moe, "rw_nat", [E, D])
        rwT = sb(moe, "rwT", [P, E])
        rb_rows = sb(moe, "rb_rows", [P, E])
        turn_i = sb(moe, "turn_i", [P, E], I32)
        turn = sb(moe, "turn", [P, E])
        sel_plain = sb(moe, "sel_plain", [P, E // 2, P])
        sel = sb(moe, "sel", [P, E // 2, P], F32R)
        score = sb(moe, "score", [P, T, E])
        sfc = sb(moe, "sfc", [P, T, E])
        ra = sb(moe, "ra", [P, T, E])
        rb = sb(moe, "rb", [P, T, E])
        rc = sb(moe, "rc", [P, T, E])
        g1 = sb(moe, "g1", [P, T, N_EGROUP])
        g2 = sb(moe, "g2", [P, T, N_EGROUP])
        g3 = sb(moe, "g3", [P, T, N_EGROUP])
        gr = sb(moe, "gr", [P, T, N_EGROUP])
        r1 = sb(moe, "r1", [P, T])
        w_cat = sb(moe, "w_cat", [P, 4, P])
        w_r = sb(moe, "w_r", [P, T, E], F32R)
        wT = sb(moe, "wT", [P, T * P], F32R)
        act_g = sb(moe, "act_g", [P, 2, BANK])
        gu_mul = sb(moe, "gu_mul", [P, 2, BANK])
        hid = sb(moe, "hid", [P, 3, BANK])

        st = stack.enter_context(nc.psum_tensor("st", [P, 2, 2, BANK], F32))
        op = stack.enter_context(nc.psum_tensor("op", [P, 2, BANK], F32))
        side = stack.enter_context(nc.psum_tensor("side", [P, 2, BANK], F32))

        s_x = sem("x_landed")
        s_w = sem("attn_weights_landed")
        s_nat = [sem("context_landed_even"), sem("context_landed_odd")]
        s_id = sem("identity_ready")
        s_set = sem("buffers_preset")
        s_link = sem("vector_step_done")
        s_plink = sem("pool_step_done")
        s_var = sem("variances_ready")
        s_std = sem("deviations_ready")
        s_xn = sem("tokens_normalised")
        s_xt = sem("tokens_turned")
        s_xT = sem("turned_tokens_kept")
        s_wt = sem("weights_turned")
        s_wT = sem("turned_weights_kept")
        s_ab = sem("weight_products_made")
        s_abk = sem("weight_products_kept")
        s_As = sem("A_staged")
        s_cs = sem("context_staged")
        s_cf = sem("context_turned")
        s_ch = sem("context_hi_kept")
        s_cd = sem("context_lo_kept")
        s_v = sem("values_split")
        s_qf = sem("queries_projected")
        s_qh = sem("queries_hi_kept")
        s_qd = sem("queries_lo_kept")
        s_mf = sem("max_scores_made")
        s_md = sem("max_scores_reduced")
        s_mc = sem("maxima_combined")
        s_tf = sem("maxima_turned")
        s_td = sem("maxima_kept")
        s_ml = sem("maxima_row_landed")
        s_qk = sem("scores_made")
        s_ex = sem("probabilities_made")
        s_lo = sem("probabilities_lo_kept")
        s_pv = sem("output_accumulated")
        s_oe = sem("output_kept")
        s_yf = sem("head_outputs_projected")
        s_yd = sem("head_outputs_added")
        s_mw = sem("moe_weights_landed")
        s_mp = sem("moe_constants_ready")
        s_kt = sem("moe_weights_turned")
        s_kh = sem("moe_weights_hi_kept")
        s_kd = sem("moe_weights_kept")
        s_lg = sem("router_logits_made")
        s_ls = sem("router_exponentials_kept")
        s_x2f = sem("x2_plain_and_hi_kept")
        s_vh = sem("values_hi_kept")
        s_st = sem("statistics_ready")
        s_rc = sem("heads_added_step")
        s_gm = sem("gate_times_up_made")
        s_rt = sem("routing_weights_made")
        s_wf = sem("routing_weights_turned")
        s_wk = sem("turned_routing_weights_kept")
        s_ga = sem("gate_made")
        s_up = sem("up_and_weights_made")
        s_si = sem("gate_activated")
        s_hd = sem("hidden_made")
        s_dn = sem("hidden_projected")
        s_fin = sem("chunk_finished")
        s_out = sem("chunk_stored")

        x_tok = x.rearrange("b (q p) d -> p (b q) d", p=P)
        out_tok = out.rearrange("b (q p) d -> p (b q) d", p=P)
        both = lambda t: t.rearrange("p a b -> p (a b)")

        a_ps, b_ps = (side[:, 1, :], op[:, 1, :]), (op[:, 0, :], st[:, 0, 1, :])

        def rows(s):
            return P if s < FULL else TAIL

        def groups(eng, body, before=None):
            with eng.Fori(0, B // 2) as bb:
                for par in range(2):
                    if before:
                        before(eng.snap(bb * 2 + par), bb, par)
                    with eng.Fori(0, NGB) as i:
                        body(eng.snap(bb * (2 * NGB) + (par * NGB) + i), bb * 2 + par, i, par)

        wturns = []
        hi_kept, lo_kept = 0, 1
        for lo in range(0, 3 * NP, 4):
            hi = min(lo + 4, 3 * NP)
            cut = min(max(2 * NP, lo), hi)
            hi_kept += (cut > lo) + (hi > cut)
            lo_kept += cut > lo
            wturns.append((lo, cut, hi, hi_kept, lo_kept))

        def after_attention(eng):
            eng.wait_ge(s_yd, 2 * NG + 2)
            eng.wait_ge(s_v, NG + NGB)
            eng.wait_ge(s_As, NG + 1)
            eng.wait_ge(s_ml, 16 * NG + 16)
            for par in range(2):
                eng.wait_ge(s_nat[par], 48 * (B // 2 + 1))

        block = stack.enter_context(nc.Block())

        @block.sync
        def _(sp):
            sp.dma_start(x1[:, 2:T + 2, :], x_tok).then_inc(s_x, 16)

            def load_context(batch, par):
                src = ctx[batch, 0:FULL * P, :].rearrange("(p t) d -> p t d", t=FULL)
                sp.dma_start(nat[:, par, 0:FULL, :], src).then_inc(s_nat[par], 16)
                sp.dma_start(nat[0:TAIL, par, FULL, :], ctx[batch, FULL * P:NC, :]).then_inc(s_nat[par], 16)
                sp.dma_start(nat[TAIL:TAIL + DOUBLES, par, FULL, :],
                             ctx[batch, 0:DOUBLES, :]).then_inc(s_nat[par], 16)

            sp.wait_ge(s_set, 1)
            load_context(0, 0)
            sp.dma_start(Wq_sb[:, :], Wq).then_inc(s_w, 16)
            sp.dma_start(Wk_sb[:, :], Wk).then_inc(s_w, 16)
            sp.dma_start(Wv_sb[:, :], Wv).then_inc(s_w, 16)
            sp.dma_start(Wo_sb[:, :, :], Wo.rearrange("(c p) n -> p c n", p=P)).then_inc(s_w, 16)
            sp.dma_start(bo_rows[:, :], bo.rearrange("(a d) -> a d", a=1).to_broadcast([P, D])).then_inc(s_w, 16)
            load_context(1, 1)

            def send_max_row(count, slot):
                sp.wait_ge(s_td, count + 1)
                sp.dma_start(qT_hi[DC:OW, slot, :].bitcast(F32).rearrange("o (a b) -> o a b", b=P),
                             m_row[:, :].bitcast(F32)).then_inc(s_ml, 16)

            send_max_row(0, 0)

            def before(b, bb, par):
                sp.wait_ge(s_v, b * NGB + NGB)
                sp.wait_ge(s_cs, b * NGB + NGB)
                load_context((bb * 2 + (par + 2)) % B, par)

            def body(G, b, i, par):
                send_max_row(G + 1, (i + 1) % 2)

            groups(sp, body, before)

            after_attention(sp)
            for k, (w, shared) in enumerate(((gate_w, sh_gate_w), (up_w, sh_up_w))):
                for two in range(2):
                    src = w.rearrange("(c t) i h -> t i c h", t=2)[two]
                    sp.dma_start(w_nat[two * EI:(two + 1) * EI, k, 0:NP - 1, :], src).then_inc(s_mw, 16)
                sp.dma_start(w_nat[:, k, NP - 1, :], shared).then_inc(s_mw, 16)
            sp.dma_start(w_nat[:, 2, 0:NP - 1, :].rearrange("p c (t i) -> p (c t) i", t=2),
                         down_w.rearrange("e h i -> h e i")).then_inc(s_mw, 16)
            sp.dma_start(w_nat[:, 2, NP - 1, :], sh_down_w).then_inc(s_mw, 16)
            sp.dma_start(rw_nat[:, :], router_w).then_inc(s_mw, 16)
            sp.dma_start(rb_rows[:, :], router_b.rearrange("(a e) -> a e", a=1).to_broadcast([P, E])).then_inc(s_mw, 16)

            with sp.Fori(0, NCH) as c:
                sp.wait_ge(s_fin, c + 1)
                sp.dma_start(out_tok[:, bass.ds(c * 4, 4), :], x1[:, bass.ds(c * 4 + 2, 4), :]).then_inc(s_out, 16)
            sp.wait_ge(s_out, 16 * NCH)

        @block.gpsimd
        def _(pool):
            steps = [0]

            def link(ins):
                steps[0] += 1
                ins.then_inc(s_plink, 1)
                pool.wait_ge(s_plink, steps[0])

            link(pool.memset(ident[:, :], 0.0))
            pool.affine_select(out=ident[:, :], in_=ident[:, :], compare_op=ALU.not_equal, fill=1.0,
                               base=0, pattern=[[-1, P]], channel_multiplier=1).then_inc(s_id, 1)
            pool.wait_ge(s_id, 1)

            def stage_A(count, g):
                pool.wait_ge(s_qf, count)
                pool.tensor_copy(A_stage[:, :, :], A_all[:, bass.ds(g * GH, GH), :]).then_inc(s_As, 1)

            def quarter(count, i, par):
                tiles = bass.ds(i * QT, QT)
                pool.wait_ge(s_cf, count)
                pool.tensor_copy(c_stage[:, :, :], nat[:, par, tiles, :]).then_inc(s_cs, 1)

            def split_values(count, i, par):
                tiles = bass.ds(i * QT, QT)
                pool.tensor_copy(v_hi[:, par, tiles, 0:DC], nat[:, par, tiles, :]).then_inc(s_vh, 1)
                pool.wait_ge(s_vh, count + 1)
                pool.tensor_tensor(v_lo[:, par, tiles, 0:DC], nat[:, par, tiles, :],
                                   v_hi[:, par, tiles, 0:DC].bitcast(F32), ALU.subtract).then_inc(s_v, 1)

            pool.wait_ge(s_nat[0], 48)
            with pool.Fori(0, NGB) as i:
                quarter(i, i, 0)
                split_values(i, i, 0)
            pool.wait_ge(s_abk, H // 2)
            stage_A(0, 0)

            def body(G, b, i, par):
                stage_A(G + 1, (i + 1) % NGB)
                pool.wait_ge(s_nat[1 - par], (b // 2) * 48 + 48 * (par + 1))
                quarter(G + NGB, i, 1 - par)
                pool.wait_ge(s_pv, G * S)
                split_values(G + NGB, i, 1 - par)

            groups(pool, body)

            after_attention(pool)
            link(pool.memset(sel_plain[:, :, :], 0.0))
            pick = sel_plain[:, :, :].rearrange("p c (t i) -> p c t i", t=2)
            for base in (0, -E):
                link(pool.affine_select(out=pick, in_=pick, compare_op=ALU.not_equal, fill=1.0, base=base,
                                        pattern=[[-2, E // 2], [-1, 2], [0, EI]], channel_multiplier=1))
            pool.tensor_copy(sel[:, :, :], sel_plain[:, :, :]).then_inc(s_mp, 1)
            link(pool.iota(turn_i[:, :], pattern=[[-1, E]], base=E, channel_multiplier=0))
            pool.tensor_copy(turn[:, :], turn_i[:, :]).then_inc(s_mp, 1)
            pool.memset(w_cat[:, :, 2 * E:P], 0.0).then_inc(s_mp, 1)

        @block.tensor
        def _(pe):
            pe.wait_ge(s_id, 1)

            def turn_tokens(count, keep_psum=st):
                for u in range(2):
                    k = count + u
                    pe.wait_ge(s_xn, k + 1)
                    if u == 0:
                        pe.wait_ge(s_xT, count)
                    for t in range(4):
                        mm = pe.transpose(st[:, u, 0, t * P:(t + 1) * P], xn[:, u, t, :], ident[:, :])
                    mm.then_inc(s_xt, 1)

            with pe.Fori(0, NCH // 2) as k:
                turn_tokens(k * 2)

            pe.wait_ge(s_w, 80)
            for c in range(H // 2):
                if c:
                    pe.wait_ge(s_abk, c)
                cols = slice(c * P, (c + 1) * P)
                pe.transpose(side[:, 0, 0:P], Wq_sb[:, cols], ident[:, :])
                pe.transpose(side[:, 0, P:P + DC], Wk_sb[:, cols], ident[0:DC, 0:DC])
                pe.transpose(side[:, 0, 2 * P:2 * P + DC], Wv_sb[:, cols],
                             ident[0:DC, 0:DC]).then_inc(s_wt, 1)
                pe.wait_ge(s_wT, c + 1)
                for j in range(2):
                    r = slice(j * DH, (j + 1) * DH)
                    pe.matmul(a_ps[j][:, 0:DC], WT[r, 0, :], WT[r, 1, 0:DC], start=True, stop=True)
                    mm = pe.matmul(b_ps[j][0:DC, 0:P], WT[r, 2, 0:DC], Wo_sb[r, c, :], start=True, stop=True)
                mm.then_inc(s_ab, 1)
            pe.wait_ge(s_abk, H // 2)

            def turn_context(count):
                pe.wait_ge(s_cs, count + 1)
                for t in range(QT):
                    mm = pe.transpose(side[0:DC, 0, t * P:(t + 1) * P], c_stage[:, t, :], ident[:, :])
                mm.then_inc(s_cf, 1)

            def project_queries(g, batch):
                pe.wait_ge(s_As, g + 1)
                for h in range(GH):
                    mm = pe.matmul(side[0:DC, h // 2, (h % 2) * NQ:(h % 2 + 1) * NQ], A_stage[:, h, :],
                                   xnT[:, bass.ds(batch * NQ, NQ)], start=True, stop=True)
                mm.then_inc(s_qf, 1)

            def max_scores(g, k, par):
                pe.wait_ge(s_md, g * NM + k)
                if k == 0:
                    pe.wait_ge(s_qh, g * 2 + 2)
                for j in range(2):
                    mm = pe.matmul(side[:, j, 0:MAXW], qT_max[:, (k // 2) * P:(k // 2 + 1) * P],
                                   cT_hi[0:DC, par, ((k % 2) * 2 + j) * MAXW:((k % 2) * 2 + j + 1) * MAXW],
                                   start=True, stop=True)
                mm.then_inc(s_mf, 1)

            def turn_maxima(g):
                pe.wait_ge(s_mc, g + 1)
                pe.transpose(side[0:NM // 2, 0, 0:P], m_neg[:, :], ident[:, :]).then_inc(s_tf, 1)

            with pe.Fori(0, NGB) as i:
                pe.wait_ge(s_cd, i)
                turn_context(i)
            pe.wait_ge(s_cd, NGB)
            pe.wait_ge(s_set, 11)
            pe.wait_ge(s_xT, NCH)
            project_queries(0, 0)
            pe.wait_ge(s_qd, 1)
            for k in range(NM):
                max_scores(0, k, 0)
            turn_maxima(0)

            def scores(G, s, i, par):
                m = rows(s)
                keys = slice(s * P, s * P + m)
                for j in range(2):
                    cols = slice(j * BANK, (j + 1) * BANK)
                    o = st[0:m, s % 2, j, :]
                    pe.matmul(o, cT_hi[:, par, keys], qT_hi[:, i % 2, cols], start=True, stop=False)
                    pe.matmul(o, cT_hi[0:DC, par, keys], qT_lo[:, i % 2, cols], start=False, stop=False)
                    mm = pe.matmul(o, cT_lo[:, par, keys], qT_hi[0:DC, i % 2, cols], start=False, stop=True)
                mm.then_inc(s_qk, 1)

            def weigh(s, par):
                m = rows(s)
                for j in range(2):
                    cols = slice(j * BANK, (j + 1) * BANK)
                    o = op[0:OW, j, :]
                    pe.matmul(o, v_hi[0:m, par, s, :], p_hi[0:m, s % 4, cols], start=(s == 0), stop=False)
                    pe.matmul(o, v_hi[0:m, par, s, :], p_lo[0:m, s % 4, cols], start=False, stop=False)
                    mm = pe.matmul(o, v_lo[0:m, par, s, :], p_hi[0:m, s % 4, cols], start=False,
                                   stop=(s == S - 1))
                mm.then_inc(s_pv, 1)

            def project_heads(count, k, g):
                for h in range(2 * k, 2 * k + 2):
                    for q in range(2):
                        at = h * NQ + q * P
                        mm = pe.matmul(side[:, h % 2, q * YW:(q + 1) * YW], oT[:, at:at + P],
                                       B_all[:, g * GH + h, :], start=True, stop=True)
                mm.then_inc(s_yf, 1)

            def body(G, b, i, par):
                n = pe.snap(G * S)

                def qk(s):
                    if s == 0:
                        pe.wait_ge(s_qd, G + 1)
                        pe.wait_ge(s_ml, G * 16 + 16)
                        pe.wait_ge(s_ex, n)
                    elif s >= 2:
                        pe.wait_ge(s_ex, n + (s - 1))
                    scores(G, s, i, par)

                def pv(s):
                    if s == 0:
                        pe.wait_ge(s_v, b * NGB + NGB)
                        pe.wait_ge(s_oe, G)
                    pe.wait_ge(s_lo, n + (s + 1))
                    weigh(s, par)

                qk(0)
                pe.wait_ge(s_td, G + 1)
                turn_context(G + NGB)
                qk(1)
                pe.wait_ge(s_cd, G + (NGB + 1))
                project_queries(G + 1, bb_next(b, i))
                qk(2)
                pv(0)
                qk(3)
                pe.wait_ge(s_qd, G + 2)
                pe.wait_ge(s_oe, G)
                project_heads(G * 2, 0, (i + (NGB - 1)) % NGB)
                pv(1)
                pe.wait_ge(s_yd, G * 2 + 1)
                project_heads(G * 2 + 1, 1, (i + (NGB - 1)) % NGB)
                k = 0
                next_par = (par + (i + 1) // NGB) % 2
                for s in range(4, S):
                    qk(s)
                    if k < NM:
                        if k == 0:
                            pe.wait_ge(s_yd, G * 2 + 2)
                        max_scores(G + 1, k, next_par)
                        k += 1
                    pv(s - 2)
                    if k < NM:
                        max_scores(G + 1, k, next_par)
                        k += 1
                turn_maxima(G + 1)
                pv(S - 2)
                pv(S - 1)

            def bb_next(b, i):
                return b + (i + 1) // NGB

            groups(pe, body)

            pe.wait_ge(s_td, NG + 1)
            pe.wait_ge(s_oe, NG)
            project_heads(2 * NG, 0, NGB - 1)
            pe.wait_ge(s_yd, 2 * NG + 1)
            project_heads(2 * NG + 1, 1, NGB - 1)
            pe.wait_ge(s_yd, 2 * NG + 2)

            pe.wait_ge(s_mw, 160)
            turns = [(k, c) for k in range(3) for c in range(NP)]
            pe.transpose(side[:, 0, 0:E], rw_nat[:, :], ident[0:E, 0:E]).then_inc(s_kt, 1)
            for j, (lo, cut, hi, _, _) in enumerate(wturns):
                if j >= 2:
                    pe.wait_ge(s_kh, wturns[j - 2][3])
                    pe.wait_ge(s_kd, wturns[j - 2][4])
                for t, (k, c) in enumerate(turns[lo:hi]):
                    mm = pe.transpose(op[:, j % 2, t * P:(t + 1) * P], w_nat[:, k, c, :], ident[:, :])
                mm.then_inc(s_kt, 1)

            with pe.Fori(0, NCH // 2) as k:
                turn_tokens(k * 2 + NCH)
                for u in range(2):
                    pe.wait_ge(s_x2f, (k * 2 + (u + 1)) * 2)
                    pe.wait_ge(s_ls, k * 2 + u)
                    for t in range(4):
                        mm = pe.matmul(side[:, 0, t * E:(t + 1) * E], x2T_f[:, u, t * P:(t + 1) * P],
                                       rwT[:, :], start=True, stop=True)
                    mm.then_inc(s_lg, 1)

            for c in range(NCH):
                pe.wait_ge(s_rt, c + 1)
                if c:
                    pe.wait_ge(s_wk, c)
                for t in range(4):
                    mm = pe.transpose(side[:, 1, t * P:(t + 1) * P], w_cat[:, t, :], ident[:, :])
                mm.then_inc(s_wf, 1)
            pe.wait_ge(s_wk, NCH)

            gate_ps, up_ps, rep_ps = st[:, 0], st[:, 1], side

            with pe.Fori(0, NCH) as c:
                n = pe.snap(c * NP)
                chunk = bass.ds(c * BANK, BANK)

                def three(o, k, p):
                    pe.matmul(o, gu_hi[:, k, p, :], x2T_hi[:, chunk], start=True, stop=False)
                    pe.matmul(o, gu_hi[:, k, p, :], x2T_lo[:, chunk], start=False, stop=False)
                    return pe.matmul(o, gu_lo[:, k, p, :], x2T_hi[:, chunk], start=False, stop=True)

                def down(p):
                    pe.wait_ge(s_hd, n + (p + 1))
                    if p == 0:
                        pe.wait_ge(s_fin, c)
                    for t in range(4):
                        mm = pe.matmul(op[:, 0, t * P:(t + 1) * P], hid[:, p % 3, t * P:(t + 1) * P],
                                       dT[:, p, :], start=(p == 0 and t == 0), stop=(p == NP - 1),
                                       skip_group_check=True)
                    mm.then_inc(s_dn, 1)

                for p in range(NP):
                    if p != 1:
                        pe.wait_ge(s_si, n + max(p - 1, 0))
                    three(gate_ps[:, p % 2, :], 0, p).then_inc(s_ga, 1)
                    if p != 1:
                        pe.wait_ge(s_hd, n + max(p - 1, 0))
                    mm = three(up_ps[:, p % 2, :], 1, p)
                    if p < NP - 1:
                        mm = pe.matmul(rep_ps[:, p % 2, :], sel[:, p, :], wT[:, chunk], start=True, stop=True)
                    mm.then_inc(s_up, 1)
                    if p >= 1:
                        down(p - 1)
                down(NP - 1)

        @block.scalar
        def _(act):
            act.wait_ge(s_var, 1)
            act.activation(std[:, :], var[:, :], ACT.Sqrt).then_inc(s_std, 1)
            with act.Fori(0, NCH // 2) as k:
                for u in range(2):
                    act.wait_ge(s_xt, k * 2 + (u + 1))
                    act.activation(xnT[:, bass.ds(k * (2 * BANK) + u * BANK, BANK)], st[:, u, 0, :],
                                   ACT.Copy).then_inc(s_xT, 1)

            def context_hi(count, i, par):
                act.wait_ge(s_cf, count + 1)
                act.activation(cT_hi[0:DC, par, bass.ds(i * BANK, BANK)], side[0:DC, 0, :],
                               ACT.Copy).then_inc(s_ch, 1)

            def queries_hi(g, slot):
                act.wait_ge(s_qf, g + 1)
                act.activation(qT_max[:, :], both(side[0:DC, :, :]), ACT.Copy).then_inc(s_qh, 1)
                act.activation(qT_hi[0:DC, slot, :], both(side[0:DC, :, :]), ACT.Copy).then_inc(s_qh, 1)

            act.wait_ge(s_set, 11)
            with act.Fori(0, NGB) as i:
                context_hi(i, i, 0)
            queries_hi(0, 0)

            def body(G, b, i, par):
                n = act.snap(G * S)

                def exp(s):
                    m = rows(s)
                    act.wait_ge(s_qk, n + (s + 1))
                    if s >= 2:
                        act.wait_ge(s_lo, n + (s - 1))
                    act.activation(p_full[0:m, s % 2, :], both(st[0:m, s % 2]), ACT.Exp, scale=SCALE)
                    if s >= 4:
                        act.wait_ge(s_pv, n + (s - 3))
                    act.activation(p_hi[0:m, s % 4, :], both(st[0:m, s % 2]), ACT.Exp,
                                   scale=SCALE).then_inc(s_ex, 1)

                exp(0)
                context_hi(G + NGB, i, 1 - par)
                exp(1)
                queries_hi(G + 1, (i + 1) % 2)
                for s in range(2, S):
                    exp(s)
                act.wait_ge(s_pv, n + S)
                act.activation(oT[:, :], both(op[0:OW]), ACT.Copy).then_inc(s_oe, 1)

            groups(act, body)

            after_attention(act)
            act.wait_ge(s_var, 2)
            act.activation(std[:, :], var[:, :], ACT.Sqrt).then_inc(s_std, 1)
            for j, (lo, cut, hi, _, _) in enumerate(wturns):
                act.wait_ge(s_kt, j + 2)
                gu = gu_hi[:, :, :, :].rearrange("p a b c -> p (a b) c")
                src = op[:, j % 2, :].rearrange("p (a b) -> p a b", b=P)
                if cut > lo:
                    act.activation(gu[:, lo:cut, :], src[:, 0:cut - lo, :], ACT.Copy).then_inc(s_kh, 1)
                if hi > cut:
                    act.activation(dT[:, cut - 2 * NP:hi - 2 * NP, :], src[:, cut - lo:hi - lo, :],
                                   ACT.Copy).then_inc(s_kh, 1)

            with act.Fori(0, NCH // 2) as k:
                for u in range(2):
                    act.wait_ge(s_xt, k * 2 + (NCH + u + 1))
                    act.wait_ge(s_lg, k * 2)
                    act.activation(x2T_f[:, u, :], st[:, u, 0, :], ACT.Copy).then_inc(s_x2f, 1)
                    act.activation(x2T_hi[:, bass.ds(k * (2 * BANK) + u * BANK, BANK)], st[:, u, 0, :],
                                   ACT.Copy).then_inc(s_x2f, 1)
                for u in range(2):
                    act.wait_ge(s_lg, k * 2 + (u + 1))
                    act.activation(score[:, bass.ds(k * 8 + u * 4, 4), :],
                                   side[:, 0, 0:4 * E].rearrange("p (a b) -> p a b", b=E),
                                   ACT.Exp, scale=-1.0).then_inc(s_ls, 1)

            for c in range(NCH):
                act.wait_ge(s_wf, c + 1)
                act.activation(wT[:, c * BANK:(c + 1) * BANK], side[:, 1, :], ACT.Copy).then_inc(s_wk, 1)

            with act.Fori(0, NCH) as c:
                n = act.snap(c * NP)
                for p in range(NP):
                    act.wait_ge(s_ga, n + (p + 1))
                    if p != 1:
                        act.wait_ge(s_hd, n + max(p - 1, 0))
                    act.activation(act_g[:, p % 2, :], st[:, 0, p % 2, :], ACT.Silu).then_inc(s_si, 1)

        @block.vector
        def _(dve):
            steps = [0]

            def link(ins):
                steps[0] += 1
                ins.then_inc(s_link, 1)
                dve.wait_ge(s_link, steps[0])

            def layernorm_stats(base, count):
                with dve.Fori(0, T) as t:
                    dve.bn_stats(stats[:, t, :], x1[:, t + 2, :]).then_inc(s_st, 1)
                dve.wait_ge(s_st, T * count)
                me, m2e, mo, m2o = (stats[:, :, j] for j in (1, 2, 4, 5))
                link(dve.tensor_tensor(mean[:, :], me, mo, ALU.add))
                link(dve.tensor_scalar(mean[:, :], mean[:, :], 0.5, None, ALU.mult))
                link(dve.tensor_tensor(dif[:, :], me, mo, ALU.subtract))
                link(dve.tensor_tensor(dif[:, :], dif[:, :], dif[:, :], ALU.mult))
                link(dve.tensor_tensor(var[:, :], m2e, m2o, ALU.add))
                link(dve.tensor_scalar(var[:, :], var[:, :], 1.0 / D, EPS, ALU.mult, ALU.add))
                dve.scalar_tensor_tensor(var[:, :], dif[:, :], 0.25, var[:, :], ALU.mult,
                                         ALU.add).then_inc(s_var, 1)
                dve.wait_ge(s_std, count)
                link(dve.reciprocal(rstd[:, :], std[:, :]))

            def normalise(k, u, base):
                dve.wait_ge(s_xt, k * 2 + base)
                for t in range(4):
                    tile = k * 8 + (u * 4 + t)
                    ins = dve.tensor_scalar(xn[:, u, t, :], x1[:, tile + 2, :], mean[:, bass.ds(tile, 1)],
                                            rstd[:, bass.ds(tile, 1)], ALU.subtract, ALU.mult)
                ins.then_inc(s_xn, 1)

            for k, (ap, value) in enumerate((
                    (nat[:, :, :, :], 0.0), (B_all[DC:OW, :, :], 0.0), (cT_hi[DC:OW, :, :].bitcast(F32), 1.0),
                    (v_hi[:, :, :, DC:OW].bitcast(F32), 1.0), (v_lo[:, :, :, DC:OW].bitcast(F32), 0.0),
                    (xnT[:, B * NQ:(B + 1) * NQ], 0.0), (oT[0:DC, :], 0.0), (oT[DC:OW, :], 1.0),
                    (x1[:, 0:2, :], 0.0), (B_all[0:DC, :, D:YW], 0.0))):
                dve.memset(ap, value).then_inc(s_set, 1)
            dve.wait_ge(s_set, 2)
            dve.memset(B_all[DC:OW, :, D:YW], 1.0).then_inc(s_set, 1)

            dve.wait_ge(s_x, 16)
            layernorm_stats(0, 1)
            with dve.Fori(0, NCH // 2) as k:
                for u in range(2):
                    normalise(k, u, 0)
            dve.wait_ge(s_w, 80)
            dve.wait_ge(s_xn, NCH)
            link(dve.tensor_tensor(x1[:, 2:T + 2, :], x1[:, 2:T + 2, :],
                                   bo_rows[:, :].rearrange("p (a d) -> p a d", a=1).to_broadcast([P, T, D]), ALU.add))

            for c in range(H // 2):
                dve.wait_ge(s_wt, c + 1)
                dve.tensor_copy(WT[:, 0, :], side[:, 0, 0:P])
                dve.tensor_copy(WT[:, 1, 0:DC], side[:, 0, P:P + DC])
                dve.tensor_copy(WT[:, 2, 0:DC], side[:, 0, 2 * P:2 * P + DC]).then_inc(s_wT, 1)
                if c == 0:
                    dve.wait_ge(s_set, 11)
                dve.wait_ge(s_ab, c + 1)
                for j in range(2):
                    dve.tensor_copy(A_all[:, 2 * c + j, :], a_ps[j][:, 0:DC])
                    ins = dve.tensor_copy(B_all[0:DC, 2 * c + j, 0:D], b_ps[j][0:DC, 0:P])
                ins.then_inc(s_abk, 1)

            def context_lo(count, i, par):
                dve.wait_ge(s_ch, count + 1)
                cols = bass.ds(i * BANK, BANK)
                dve.tensor_tensor(cT_lo[:, par, cols], side[0:DC, 0, :],
                                  cT_hi[0:DC, par, cols].bitcast(F32), ALU.subtract).then_inc(s_cd, 1)

            def queries_lo(g, slot):
                dve.wait_ge(s_qh, g * 2 + 2)
                dve.tensor_tensor(qT_lo[:, slot, :], both(side[0:DC, :, :]),
                                  qT_max[:, :].bitcast(F32), ALU.subtract).then_inc(s_qd, 1)

            def reduce_max(g, k):
                dve.wait_ge(s_mf, g * NM + (k + 1))
                dve.tensor_reduce(m_part[:, k:k + 1], side[:, :, 0:MAXW], AX.XY, ALU.max).then_inc(s_md, 1)

            def combine_max(g):
                dve.wait_ge(s_md, g * NM + NM)
                dve.tensor_reduce(m_neg[:, :], m_part[:, :].rearrange("p (a b) -> p a b", b=2), AX.X,
                                  ALU.max, negate=True).then_inc(s_mc, 1)

            def keep_max_rows(g):
                dve.wait_ge(s_tf, g + 1)
                dve.wait_ge(s_ml, g * 16)
                dve.tensor_copy(m_row[:, :], side[0:NM // 2, 0, 0:P]).then_inc(s_td, 1)

            def add_heads(count, batch1):
                dve.wait_ge(s_yf, count + 1)
                ys = side[:, :, 0:2 * YW].rearrange("p a (q y) -> p a q y", q=2)
                dve.reciprocal(recip[:, :].rearrange("p (a q y) -> p a q y", a=2, q=2),
                               ys[:, :, :, D:YW]).then_inc(s_rc, 1)
                dve.wait_ge(s_rc, count * 3 + 1)
                for h in range(2):
                    for q in range(2):
                        tile = batch1 * 2 + q
                        ins = dve.scalar_tensor_tensor(x1[:, tile, :], ys[:, h, q, 0:D],
                                                       recip[:, 2 * h + q:2 * h + q + 1], x1[:, tile, :],
                                                       ALU.mult, ALU.add)
                    if h == 0:
                        ins.then_inc(s_rc, 1)
                        dve.wait_ge(s_rc, count * 3 + 2)
                ins.then_inc(s_rc, 1)
                dve.wait_ge(s_rc, count * 3 + 3)
                dve.sem_inc(s_yd, 1)

            with dve.Fori(0, NGB) as i:
                context_lo(i, i, 0)
            queries_lo(0, 0)
            for k in range(NM):
                reduce_max(0, k)
            combine_max(0)
            keep_max_rows(0)

            def body(G, b, i, par):
                n = dve.snap(G * S)

                def lo(s):
                    m = rows(s)
                    dve.wait_ge(s_ex, n + (s + 1))
                    dve.tensor_tensor(p_lo[0:m, s % 4, :], p_full[0:m, s % 2, :],
                                      p_hi[0:m, s % 4, :].bitcast(F32), ALU.subtract).then_inc(s_lo, 1)

                batch1 = b + (i + (NGB - 1)) // NGB
                lo(0)
                context_lo(G + NGB, i, 1 - par)
                lo(1)
                queries_lo(G + 1, (i + 1) % 2)
                add_heads(G * 2, batch1)
                lo(2)
                add_heads(G * 2 + 1, batch1)
                k = 0
                for s in range(4, S):
                    lo(s - 1)
                    for _ in range(2):
                        if k < NM:
                            reduce_max(G + 1, k)
                            k += 1
                    if k == NM:
                        k += 1
                        combine_max(G + 1)
                keep_max_rows(G + 1)
                lo(S - 1)

            groups(dve, body)
            add_heads(2 * NG, B)
            add_heads(2 * NG + 1, B)

            after_attention(dve)
            layernorm_stats(1, 2)
            dve.wait_ge(s_kt, 1)
            dve.tensor_copy(rwT[:, :], side[:, 0, 0:E]).then_inc(s_kd, 1)
            fh = gu_hi[:, :, :, :].rearrange("p a b c -> p (a b) c")
            fl = gu_lo[:, :, :, :].rearrange("p a b c -> p (a b) c")
            for j, (lo, cut, hi, kept, _) in enumerate(wturns):
                if cut > lo:
                    dve.wait_ge(s_kh, kept)
                    src = op[:, j % 2, :].rearrange("p (a b) -> p a b", b=P)
                    dve.tensor_tensor(fl[:, lo:cut, :], src[:, 0:cut - lo, :],
                                      fh[:, lo:cut, :].bitcast(F32), ALU.subtract).then_inc(s_kd, 1)
            with dve.Fori(0, NCH // 2) as k:
                for u in range(2):
                    normalise(k, u, NCH)
                for u in range(2):
                    dve.wait_ge(s_x2f, (k * 2 + (u + 1)) * 2)
                    cols = bass.ds(k * (2 * BANK) + u * BANK, BANK)
                    dve.tensor_tensor(x2T_lo[:, cols], st[:, u, 0, :], x2T_hi[:, cols].bitcast(F32),
                                      ALU.subtract).then_inc(s_xT, 1)

            dve.wait_ge(s_ls, NCH)
            dve.wait_ge(s_mp, 3)
            by_group = lambda t: t.rearrange("p t (g e) -> p (t g) e", g=N_EGROUP)
            flat = lambda t: t.rearrange("p t g -> p (t g)")
            wide = lambda t, e: flat(t).rearrange("p (a b) -> p a b", b=1).to_broadcast([P, T * N_EGROUP, e])
            tok = lambda t: t.rearrange("p (a b) -> p a b", b=1).to_broadcast([P, T, E])
            exp = lambda t: t.rearrange("p (a b) -> p a b", a=1).to_broadcast([P, T, E])
            EG = E // N_EGROUP
            link(dve.tensor_scalar(ra[:, :, :], score[:, :, :], 1.0, None, ALU.add))
            link(dve.reciprocal(score[:, :, :], ra[:, :, :]))
            link(dve.tensor_tensor(sfc[:, :, :], score[:, :, :], exp(rb_rows[:, :]), ALU.add))
            link(dve.tensor_reduce(flat(g1[:, :, :]), by_group(sfc[:, :, :]), AX.X, ALU.max))
            link(dve.tensor_tensor(by_group(ra[:, :, :]), by_group(sfc[:, :, :]), wide(g1[:, :, :], EG), ALU.is_equal))
            link(dve.tensor_reduce(flat(g3[:, :, :]), by_group(ra[:, :, :]), AX.X, ALU.add))
            link(dve.scalar_tensor_tensor(rb[:, :, :], ra[:, :, :], -BIG, sfc[:, :, :], ALU.mult, ALU.add))
            link(dve.tensor_reduce(flat(g2[:, :, :]), by_group(rb[:, :, :]), AX.X, ALU.max))
            link(dve.tensor_scalar(g3[:, :, :], g3[:, :, :], 1.5, None, ALU.is_gt))
            link(dve.scalar_tensor_tensor(gr[:, :, :], g3[:, :, :], -BIG * 2, g2[:, :, :], ALU.mult, ALU.add))
            link(dve.tensor_scalar(g3[:, :, :], g3[:, :, :], -1.0, BIG * 2, ALU.add, ALU.mult))
            link(dve.tensor_tensor(g3[:, :, :], g3[:, :, :], g1[:, :, :], ALU.add))
            link(dve.tensor_tensor(g2[:, :, :], g3[:, :, :], gr[:, :, :], ALU.max))
            link(dve.tensor_tensor(g1[:, :, :], g1[:, :, :], g2[:, :, :], ALU.add))
            link(dve.memset(gr[:, :, :], 0.0))
            for a in range(N_EGROUP):
                for b in range(a + 1, N_EGROUP):
                    link(dve.tensor_tensor(r1[:, :], g1[:, :, a], g1[:, :, b], ALU.is_ge))
                    link(dve.tensor_tensor(gr[:, :, b], gr[:, :, b], r1[:, :], ALU.add))
                    link(dve.tensor_scalar(r1[:, :], r1[:, :], -1.0, 1.0, ALU.mult, ALU.add))
                    link(dve.tensor_tensor(gr[:, :, a], gr[:, :, a], r1[:, :], ALU.add))
            link(dve.tensor_scalar(gr[:, :, :], gr[:, :, :], TOPK_EGROUP - 0.5, None, ALU.is_lt))
            link(dve.tensor_tensor(by_group(sfc[:, :, :]), by_group(sfc[:, :, :]), wide(gr[:, :, :], EG), ALU.mult))
            link(dve.memset(rc[:, :, :], 0.0))
            for _ in range(TOP_K):
                link(dve.tensor_reduce(r1[:, :], sfc[:, :, :], AX.X, ALU.max))
                link(dve.tensor_tensor(ra[:, :, :], sfc[:, :, :], tok(r1[:, :]), ALU.is_equal))
                link(dve.tensor_tensor(ra[:, :, :], ra[:, :, :], exp(turn[:, :]), ALU.mult))
                link(dve.tensor_reduce(r1[:, :], ra[:, :, :], AX.X, ALU.max))
                link(dve.tensor_tensor(ra[:, :, :], ra[:, :, :], tok(r1[:, :]), ALU.is_equal))
                link(dve.tensor_tensor(rc[:, :, :], rc[:, :, :], ra[:, :, :], ALU.add))
                link(dve.scalar_tensor_tensor(sfc[:, :, :], ra[:, :, :], -BIG, sfc[:, :, :], ALU.mult, ALU.add))
            link(dve.tensor_tensor(ra[:, :, :], score[:, :, :], rc[:, :, :], ALU.mult))
            link(dve.tensor_reduce(r1[:, :], ra[:, :, :], AX.X, ALU.add))
            link(dve.tensor_scalar(r1[:, :], r1[:, :], 1e-20, None, ALU.add))
            link(dve.reciprocal(r1[:, :], r1[:, :]))
            link(dve.tensor_tensor(ra[:, :, :], ra[:, :, :], tok(r1[:, :]), ALU.mult))
            link(dve.tensor_scalar(ra[:, :, :], ra[:, :, :], ROUTE_SCALE, None, ALU.mult))
            link(dve.tensor_copy(w_r[:, :, :], ra[:, :, :]))
            link(dve.tensor_tensor(rb[:, :, :], ra[:, :, :], w_r[:, :, :].bitcast(F32), ALU.subtract))
            for c in range(NCH):
                if c:
                    dve.wait_ge(s_wf, c)
                tiles = slice(4 * c, 4 * c + 4)
                link(dve.tensor_copy(w_cat[:, :, 0:E], w_r[:, tiles, :].bitcast(F32)))
                dve.tensor_copy(w_cat[:, :, E:2 * E], rb[:, tiles, :]).then_inc(s_rt, 1)

            with dve.Fori(0, NCH) as c:
                n = dve.snap(c * NP)
                for p in range(NP):
                    dve.wait_ge(s_si, n + (p + 1))
                    dve.wait_ge(s_up, n + (p + 1))
                    dve.wait_ge(s_dn, n + max(p - 1, 0))
                    if p < NP - 1:
                        dve.tensor_tensor(gu_mul[:, p % 2, :], st[:, 1, p % 2, :], act_g[:, p % 2, :],
                                          ALU.mult).then_inc(s_gm, 1)
                        dve.wait_ge(s_gm, c * (NP - 1) + (p + 1))
                        dve.tensor_tensor(hid[:, p % 3, :], side[:, p % 2, :], gu_mul[:, p % 2, :],
                                          ALU.mult).then_inc(s_hd, 1)
                    else:
                        dve.tensor_tensor(hid[:, p % 3, :], st[:, 1, p % 2, :], act_g[:, p % 2, :],
                                          ALU.mult).then_inc(s_hd, 1)
                dve.wait_ge(s_dn, n + NP)
                tiles = bass.ds(c * 4 + 2, 4)
                dve.tensor_tensor(x1[:, tiles, :], op[:, 0, :].rearrange("p (a b) -> p a b", b=P),
                                  x1[:, tiles, :], ALU.add).then_inc(s_fin, 1)


_INS = ['x', 'ctx_768', 'L0_xattn_Wq', 'L0_xattn_Wk', 'L0_xattn_Wv', 'L0_xattn_Wo', 'L0_xattn_bo',
        'L0_ffn_router_weight', 'L0_ffn_router_bias', 'L0_ffn_gate_w', 'L0_ffn_up_w', 'L0_ffn_down_w',
        'L0_ffn_shared_gate_w', 'L0_ffn_shared_up_w', 'L0_ffn_shared_down_w']


def kernel(**inputs):
    import numpy as np
    import concourse.bacc as bacc
    from concourse.bass_utils import run_bass_kernel_spmd

    nc = bacc.Bacc("TRN2", target_bir_lowering=False, num_devices=1)
    arrays, args = {}, []
    for name in _INS:
        a = np.ascontiguousarray(inputs[name])
        arrays[f"in_{name}"] = a
        args.append(nc.dram_tensor(f"in_{name}", a.shape, mybir.dt.from_np(a.dtype), kind="ExternalInput").ap())
    out = nc.dram_tensor("out_x", inputs["x"].shape, F32, kind="ExternalOutput").ap()
    xattn_moe(nc, *args, out)
    r = run_bass_kernel_spmd(nc, [arrays], core_ids=[0])
    return r.results[0]["out_x"]
```

```python
from contextlib import ExitStack

import concourse.bass as bass
from concourse import mybir

ALU = mybir.AluOpType
ACT = mybir.ActivationFunctionType
AX = mybir.AxisListType
F32 = mybir.dt.float32
F32R = mybir.dt.float32r
I32 = mybir.dt.int32

P = 128
BANK = 512
TOP_K, N_EGROUP, TOPK_EGROUP, ROUTE_SCALE = 4, 4, 2, 2.5
EPS = 1e-5
BIG = 1e30


def xattn_moe(nc, x, ctx, Wq, Wk, Wv, Wo, bo, router_w, router_b, gate_w, up_w, down_w,
              sh_gate_w, sh_up_w, sh_down_w, out):
    B, NQ, D = x.shape
    _, NC, DC = ctx.shape
    INNER = Wq.shape[1]
    DH = 64
    H = INNER // DH
    E, EI, _ = gate_w.shape
    SCALE = float(DH) ** -0.5
    assert D == P and NQ == 2 * P and H == 16 and EI * 2 == P and sh_gate_w.shape[0] == P

    GH = 4
    GQ = GH * NQ
    NGB = H // GH
    NG = B * NGB
    FULL = NC // P
    TAIL = NC - FULL * P
    S = FULL + 1
    QT = 4
    SPAD = NGB * QT
    MAXW = 402
    DOUBLES = 4 * MAXW - NC
    NM = 4 * (GQ // P)
    T = B * NQ // P
    NCH = T // 4
    NP = E // 2 + 1
    YW = D + 1
    OW = DC + 1

    stack = ExitStack()
    with stack:
        def sb(where, name, shape, dt=F32):
            return where.enter_context(nc.sbuf_tensor(name, shape, dt))

        def sem(name):
            return stack.enter_context(nc.semaphore(name))

        x1 = sb(stack, "x1", [P, T + 2, D])
        ident = sb(stack, "ident", [P, P])
        bo_rows = sb(stack, "bo_rows", [P, D])
        stats = sb(stack, "stats", [P, T, 6])
        mean = sb(stack, "mean", [P, T])
        dif = sb(stack, "dif", [P, T])
        var = sb(stack, "var", [P, T])
        std = sb(stack, "std", [P, T])
        rstd = sb(stack, "rstd", [P, T])
        xn = sb(stack, "xn", [P, 2, 4, D])
        recip = sb(stack, "recip", [P, 2])

        att = ExitStack()
        xnT = sb(att, "xnT", [P, (B + 1) * NQ])
        A_all = sb(att, "A_all", [P, H, DC])
        B_all = sb(att, "B_all", [OW, H, YW])
        A_stage = sb(att, "A_stage", [P, GH, DC])
        nat = sb(att, "nat", [P, 2, SPAD, DC])
        c_stage = sb(att, "c_stage", [P, QT, DC])
        cT_hi = sb(att, "cT_hi", [OW, 2, SPAD * P], F32R)
        cT_lo = sb(att, "cT_lo", [DC, 2, SPAD * P], F32R)
        v_hi = sb(att, "v_hi", [P, 2, SPAD, OW], F32R)
        v_lo = sb(att, "v_lo", [P, 2, SPAD, OW], F32R)
        qT_hi = sb(att, "qT_hi", [OW, 2, GQ], F32R)
        qT_lo = sb(att, "qT_lo", [DC, 2, GQ], F32R)
        qT_max = sb(att, "qT_max", [DC, GQ], F32R)
        m_part = sb(att, "m_part", [P, NM])
        m_neg = sb(att, "m_neg", [P, NM // 4])
        m_row = sb(att, "m_row", [NM // 4, P], F32R)
        oT = sb(att, "oT", [OW, GQ])
        with ExitStack() as early:
            Wq_sb = sb(early, "Wq_sb", [P, INNER])
            Wk_sb = sb(early, "Wk_sb", [DC, INNER])
            Wv_sb = sb(early, "Wv_sb", [DC, INNER])
            Wo_sb = sb(early, "Wo_sb", [P, INNER // P, D])
            WT = sb(early, "WT", [P, 3, P])
        p_full = sb(att, "p_full", [P, 2, GQ])
        p_hi = sb(att, "p_hi", [P, 4, GQ], F32R)
        p_lo = sb(att, "p_lo", [P, 4, GQ], F32R)
        att.close()

        moe = stack.enter_context(ExitStack())
        x2T_hi = sb(moe, "x2T_hi", [P, T * P], F32R)
        x2T_lo = sb(moe, "x2T_lo", [P, T * P], F32R)
        x2T_f = sb(moe, "x2T_f", [P, 2, BANK])
        w_nat = sb(moe, "w_nat", [P, 3, NP, P])
        gu_hi = sb(moe, "gu_hi", [P, 2, NP, P], F32R)
        gu_lo = sb(moe, "gu_lo", [P, 2, NP, P], F32R)
        dT = sb(moe, "dT", [P, NP, P])
        rw_nat = sb(moe, "rw_nat", [E, D])
        rwT = sb(moe, "rwT", [P, E])
        rb_rows = sb(moe, "rb_rows", [P, E])
        turn_i = sb(moe, "turn_i", [P, E], I32)
        turn = sb(moe, "turn", [P, E])
        sel_plain = sb(moe, "sel_plain", [P, E // 2, P])
        sel = sb(moe, "sel", [P, E // 2, P], F32R)
        score = sb(moe, "score", [P, T, E])
        sfc = sb(moe, "sfc", [P, T, E])
        ra = sb(moe, "ra", [P, T, E])
        rb = sb(moe, "rb", [P, T, E])
        rc = sb(moe, "rc", [P, T, E])
        g1 = sb(moe, "g1", [P, T, N_EGROUP])
        g2 = sb(moe, "g2", [P, T, N_EGROUP])
        g3 = sb(moe, "g3", [P, T, N_EGROUP])
        gr = sb(moe, "gr", [P, T, N_EGROUP])
        r1 = sb(moe, "r1", [P, T])
        w_cat = sb(moe, "w_cat", [P, 4, P])
        w_r = sb(moe, "w_r", [P, T, E], F32R)
        wT = sb(moe, "wT", [P, T * P], F32R)
        act_g = sb(moe, "act_g", [P, 2, BANK])
        gu_mul = sb(moe, "gu_mul", [P, 2, BANK])
        hid = sb(moe, "hid", [P, 3, BANK])

        st = stack.enter_context(nc.psum_tensor("st", [P, 2, 2, BANK], F32))
        op = stack.enter_context(nc.psum_tensor("op", [P, 2, BANK], F32))
        side = stack.enter_context(nc.psum_tensor("side", [P, 2, BANK], F32))

        s_x = sem("x_landed")
        s_w = sem("attn_weights_landed")
        s_nat = [sem("context_landed_even"), sem("context_landed_odd")]
        s_id = sem("identity_ready")
        s_set = sem("buffers_preset")
        s_link = sem("vector_step_done")
        s_plink = sem("pool_step_done")
        s_var = sem("variances_ready")
        s_std = sem("deviations_ready")
        s_xn = sem("tokens_normalised")
        s_xt = sem("tokens_turned")
        s_xT = sem("turned_tokens_kept")
        s_wt = sem("weights_turned")
        s_wT = sem("turned_weights_kept")
        s_ab = sem("weight_products_made")
        s_abk = sem("weight_products_kept")
        s_As = sem("A_staged")
        s_cs = sem("context_staged")
        s_fill = sem("side_job_made")
        s_drain = sem("side_job_used")
        s_ch = sem("context_hi_kept")
        s_v = sem("values_split")
        s_qh = sem("queries_hi_kept")
        s_mc = sem("maxima_combined")
        s_ml = sem("maxima_row_landed")
        s_qk = sem("scores_made")
        s_ex = sem("probabilities_made")
        s_lo = sem("probabilities_lo_kept")
        s_pv = sem("output_accumulated")
        s_oe = sem("output_kept")
        s_mw = sem("moe_weights_landed")
        s_mp = sem("moe_constants_ready")
        s_kt = sem("moe_weights_turned")
        s_kh = sem("moe_weights_hi_kept")
        s_kd = sem("moe_weights_kept")
        s_lg = sem("router_logits_made")
        s_ls = sem("router_exponentials_kept")
        s_x2f = sem("x2_plain_and_hi_kept")
        s_vh = sem("values_hi_kept")
        s_st = sem("statistics_ready")
        s_rc = sem("heads_added_step")
        s_gm = sem("gate_times_up_made")
        s_rt = sem("routing_weights_made")
        s_wf = sem("routing_weights_turned")
        s_wk = sem("turned_routing_weights_kept")
        s_ga = sem("gate_made")
        s_up = sem("up_and_weights_made")
        s_si = sem("gate_activated")
        s_hd = sem("hidden_made")
        s_dn = sem("hidden_projected")
        s_fin = sem("chunk_finished")
        s_out = sem("chunk_stored")

        x_tok = x.rearrange("b (q p) d -> p (b q) d", p=P)
        out_tok = out.rearrange("b (q p) d -> p (b q) d", p=P)
        both = lambda t: t.rearrange("p a b -> p (a b)")

        J_Q, J_C, J_M = 0, 2, 3
        J_Y = [J_M + NM, J_M + NM + 1, J_M + NM + 3, J_M + NM + 4]
        J_T = J_M + NM + 2
        JOBS = J_T + 3
        J0_Q, J0_M, J0_T = NGB, NGB + 2, NGB + 2 + NM
        JOBS0 = J0_T + 1
        assert JOBS % 2 == 0

        def bank0(j):
            return side[:, j % 2, :]

        def bank(j):
            return side[:, (JOBS0 + j) % 2, :]

        a_ps, b_ps = (side[:, 1, :], op[:, 1, :]), (op[:, 0, :], st[:, 0, 1, :])

        def rows(s):
            return P if s < FULL else TAIL

        def groups(eng, body, before=None):
            with eng.Fori(0, B // 2) as bb:
                for par in range(2):
                    if before:
                        before(eng.snap(bb * 2 + par), bb, par)
                    with eng.Fori(0, NGB) as i:
                        body(eng.snap(bb * (2 * NGB) + (par * NGB) + i), bb * 2 + par, i, par)

        wturns = []
        hi_kept, lo_kept = 0, 1
        for lo in range(0, 3 * NP, 4):
            hi = min(lo + 4, 3 * NP)
            cut = min(max(2 * NP, lo), hi)
            hi_kept += (cut > lo) + (hi > cut)
            lo_kept += cut > lo
            wturns.append((lo, cut, hi, hi_kept, lo_kept))

        def after_attention(eng):
            eng.wait_ge(s_drain, JOBS0 + JOBS * NG + GH)
            eng.wait_ge(s_v, NG + NGB)
            eng.wait_ge(s_As, NG + 1)
            eng.wait_ge(s_ml, 16 * NG + 16)
            for par in range(2):
                eng.wait_ge(s_nat[par], 48 * (B // 2 + 1))

        block = stack.enter_context(nc.Block())

        @block.sync
        def _(sp):
            sp.dma_start(x1[:, 2:T + 2, :], x_tok).then_inc(s_x, 16)

            def load_context(batch, par):
                src = ctx[batch, 0:FULL * P, :].rearrange("(p t) d -> p t d", t=FULL)
                sp.dma_start(nat[:, par, 0:FULL, :], src).then_inc(s_nat[par], 16)
                sp.dma_start(nat[0:TAIL, par, FULL, :], ctx[batch, FULL * P:NC, :]).then_inc(s_nat[par], 16)
                sp.dma_start(nat[TAIL:TAIL + DOUBLES, par, FULL, :],
                             ctx[batch, 0:DOUBLES, :]).then_inc(s_nat[par], 16)

            sp.wait_ge(s_set, 1)
            load_context(0, 0)
            sp.dma_start(Wq_sb[:, :], Wq).then_inc(s_w, 16)
            sp.dma_start(Wk_sb[:, :], Wk).then_inc(s_w, 16)
            sp.dma_start(Wv_sb[:, :], Wv).then_inc(s_w, 16)
            sp.dma_start(Wo_sb[:, :, :], Wo.rearrange("(c p) n -> p c n", p=P)).then_inc(s_w, 16)
            sp.dma_start(bo_rows[:, :], bo.rearrange("(a d) -> a d", a=1).to_broadcast([P, D])).then_inc(s_w, 16)
            load_context(1, 1)

            def send_max_row(used, slot):
                sp.wait_ge(s_drain, used)
                sp.dma_start(qT_hi[DC:OW, slot, :].bitcast(F32).rearrange("o (a b) -> o a b", b=P),
                             m_row[:, :].bitcast(F32)).then_inc(s_ml, 16)

            send_max_row(JOBS0, 0)

            def before(b, bb, par):
                sp.wait_ge(s_v, b * NGB + NGB)
                sp.wait_ge(s_cs, b * NGB + NGB)
                load_context((bb * 2 + (par + 2)) % B, par)

            def body(G, b, i, par):
                send_max_row(G * JOBS + (JOBS0 + J_T + 1), (i + 1) % 2)

            groups(sp, body, before)

            after_attention(sp)
            for k, (w, shared) in enumerate(((gate_w, sh_gate_w), (up_w, sh_up_w))):
                for two in range(2):
                    src = w.rearrange("(c t) i h -> t i c h", t=2)[two]
                    sp.dma_start(w_nat[two * EI:(two + 1) * EI, k, 0:NP - 1, :], src).then_inc(s_mw, 16)
                sp.dma_start(w_nat[:, k, NP - 1, :], shared).then_inc(s_mw, 16)
            sp.dma_start(w_nat[:, 2, 0:NP - 1, :].rearrange("p c (t i) -> p (c t) i", t=2),
                         down_w.rearrange("e h i -> h e i")).then_inc(s_mw, 16)
            sp.dma_start(w_nat[:, 2, NP - 1, :], sh_down_w).then_inc(s_mw, 16)
            sp.dma_start(rw_nat[:, :], router_w).then_inc(s_mw, 16)
            sp.dma_start(rb_rows[:, :], router_b.rearrange("(a e) -> a e", a=1).to_broadcast([P, E])).then_inc(s_mw, 16)

            with sp.Fori(0, NCH) as c:
                sp.wait_ge(s_fin, c + 2)
                sp.dma_start(out_tok[:, bass.ds(c * 4, 4), :], x1[:, bass.ds(c * 4 + 2, 4), :]).then_inc(s_out, 16)
            sp.wait_ge(s_out, 16 * NCH)

        @block.gpsimd
        def _(pool):
            steps = [0]

            def link(ins):
                steps[0] += 1
                ins.then_inc(s_plink, 1)
                pool.wait_ge(s_plink, steps[0])

            link(pool.memset(ident[:, :], 0.0))
            pool.affine_select(out=ident[:, :], in_=ident[:, :], compare_op=ALU.not_equal, fill=1.0,
                               base=0, pattern=[[-1, P]], channel_multiplier=1).then_inc(s_id, 1)
            pool.wait_ge(s_id, 1)

            def stage_A(g):
                pool.tensor_copy(A_stage[:, :, :], A_all[:, bass.ds(g * GH, GH), :]).then_inc(s_As, 1)

            def stage_context(i, par):
                pool.tensor_copy(c_stage[:, :, :], nat[:, par, bass.ds(i * QT, QT), :]).then_inc(s_cs, 1)

            def split_values(count, i, par):
                tiles = bass.ds(i * QT, QT)
                pool.tensor_copy(v_hi[:, par, tiles, 0:DC], nat[:, par, tiles, :]).then_inc(s_vh, 1)
                pool.wait_ge(s_vh, count + 1)
                pool.tensor_tensor(v_lo[:, par, tiles, 0:DC], nat[:, par, tiles, :],
                                   v_hi[:, par, tiles, 0:DC].bitcast(F32), ALU.subtract).then_inc(s_v, 1)

            pool.wait_ge(s_nat[0], 48)
            for i in range(NGB):
                if i:
                    pool.wait_ge(s_fill, i)
                stage_context(i, 0)
                split_values(i, i, 0)
            pool.wait_ge(s_abk, H // 2)
            stage_A(0)
            pool.wait_ge(s_fill, J0_Q + 2)

            def body(G, b, i, par):
                pool.wait_ge(s_fill, G * JOBS + (JOBS0 - JOBS + J_C + 1))
                stage_A((i + 1) % NGB)
                pool.wait_ge(s_nat[1 - par], (b // 2) * 48 + 48 * (par + 1))
                stage_context(i, 1 - par)
                pool.wait_ge(s_oe, G + 1)
                split_values(G + NGB, i, 1 - par)

            groups(pool, body)

            after_attention(pool)
            link(pool.memset(sel_plain[:, :, :], 0.0))
            pick = sel_plain[:, :, :].rearrange("p c (t i) -> p c t i", t=2)
            for base in (0, -E):
                link(pool.affine_select(out=pick, in_=pick, compare_op=ALU.not_equal, fill=1.0, base=base,
                                        pattern=[[-2, E // 2], [-1, 2], [0, EI]], channel_multiplier=1))
            pool.tensor_copy(sel[:, :, :], sel_plain[:, :, :]).then_inc(s_mp, 1)
            link(pool.iota(turn_i[:, :], pattern=[[-1, E]], base=E, channel_multiplier=0))
            pool.tensor_copy(turn[:, :], turn_i[:, :]).then_inc(s_mp, 1)
            pool.memset(w_cat[:, :, 2 * E:P], 0.0).then_inc(s_mp, 1)

        @block.tensor
        def _(pe):
            pe.sem_inc(s_xt, 1)
            pe.sem_inc(s_lg, 1)
            pe.wait_ge(s_id, 1)

            def turn_tokens(count):
                for u in range(2):
                    k = count + u
                    pe.wait_ge(s_xn, k + 1)
                    if u == 0:
                        pe.wait_ge(s_xT, count + 1)
                    for t in range(4):
                        mm = pe.transpose(st[:, u, 0, t * P:(t + 1) * P], xn[:, u, t, :], ident[:, :])
                    mm.then_inc(s_xt, 1)

            with pe.Fori(0, NCH // 2) as k:
                turn_tokens(k * 2)

            pe.wait_ge(s_w, 80)
            for c in range(H // 2):
                if c:
                    pe.wait_ge(s_abk, c)
                cols = slice(c * P, (c + 1) * P)
                pe.transpose(side[:, 0, 0:P], Wq_sb[:, cols], ident[:, :])
                pe.transpose(side[:, 0, P:P + DC], Wk_sb[:, cols], ident[0:DC, 0:DC])
                pe.transpose(side[:, 0, 2 * P:2 * P + DC], Wv_sb[:, cols],
                             ident[0:DC, 0:DC]).then_inc(s_wt, 1)
                pe.wait_ge(s_wT, c + 1)
                for j in range(2):
                    r = slice(j * DH, (j + 1) * DH)
                    pe.matmul(a_ps[j][:, 0:DC], WT[r, 0, :], WT[r, 1, 0:DC], start=True, stop=True)
                    mm = pe.matmul(b_ps[j][0:DC, 0:P], WT[r, 2, 0:DC], Wo_sb[r, c, :], start=True, stop=True)
                mm.then_inc(s_ab, 1)
            pe.wait_ge(s_abk, H // 2)

            def turn_context(where, count):
                pe.wait_ge(s_cs, count)
                for t in range(QT):
                    mm = pe.transpose(where[0:DC, t * P:(t + 1) * P], c_stage[:, t, :], ident[:, :])
                mm.then_inc(s_fill, 1)

            def project_queries(where, k, batch):
                for h in range(2):
                    mm = pe.matmul(where[0:DC, h * NQ:(h + 1) * NQ], A_stage[:, 2 * k + h, :],
                                   xnT[:, bass.ds(batch * NQ, NQ)], start=True, stop=True)
                mm.then_inc(s_fill, 1)

            def max_scores(where, k, par):
                pe.matmul(where[:, 0:MAXW], qT_max[:, (k // 4) * P:(k // 4 + 1) * P],
                          cT_hi[0:DC, par, (k % 4) * MAXW:(k % 4 + 1) * MAXW],
                          start=True, stop=True).then_inc(s_fill, 1)

            def turn_maxima(where, g):
                pe.wait_ge(s_mc, g + 1)
                pe.transpose(where[0:NM // 4, 0:P], m_neg[:, :], ident[:, :]).then_inc(s_fill, 1)

            def bank_free0(j):
                pe.wait_ge(s_drain, j - 1)

            for i in range(NGB):
                if i >= 2:
                    bank_free0(i)
                turn_context(bank0(i), i + 1)
            pe.wait_ge(s_set, 11)
            pe.wait_ge(s_xT, NCH + 1)
            pe.wait_ge(s_As, 1)
            for k in range(2):
                bank_free0(J0_Q + k)
                project_queries(bank0(J0_Q + k), k, 0)
            pe.wait_ge(s_qh, 4)
            for k in range(NM):
                bank_free0(J0_M + k)
                max_scores(bank0(J0_M + k), k, 0)
            bank_free0(J0_T)
            turn_maxima(bank0(J0_T), 0)

            def scores(G, s, i, par):
                m = rows(s)
                keys = slice(s * P, s * P + m)
                for j in range(2):
                    cols = slice(j * BANK, (j + 1) * BANK)
                    o = st[0:m, s % 2, j, :]
                    pe.matmul(o, cT_hi[:, par, keys], qT_hi[:, i % 2, cols], start=True, stop=False)
                    pe.matmul(o, cT_hi[0:DC, par, keys], qT_lo[:, i % 2, cols], start=False, stop=False)
                    mm = pe.matmul(o, cT_lo[:, par, keys], qT_hi[0:DC, i % 2, cols], start=False, stop=True)
                mm.then_inc(s_qk, 1)

            def weigh(s, par):
                m = rows(s)
                for j in range(2):
                    cols = slice(j * BANK, (j + 1) * BANK)
                    o = op[0:OW, j, :]
                    pe.matmul(o, v_hi[0:m, par, s, :], p_hi[0:m, s % 4, cols], start=(s == 0), stop=False)
                    pe.matmul(o, v_hi[0:m, par, s, :], p_lo[0:m, s % 4, cols], start=False, stop=False)
                    mm = pe.matmul(o, v_lo[0:m, par, s, :], p_hi[0:m, s % 4, cols], start=False,
                                   stop=(s == S - 1))
                mm.then_inc(s_pv, 1)

            def project_head(where, h, g):
                for q in range(2):
                    at = h * NQ + q * P
                    mm = pe.matmul(where[:, q * YW:(q + 1) * YW], oT[:, at:at + P],
                                   B_all[:, g * GH + h, :], start=True, stop=True)
                mm.then_inc(s_fill, 1)

            def body(G, b, i, par):
                n = pe.snap(G * S)
                jobs = pe.snap(G * JOBS + JOBS0)

                def bank_free(j):
                    pe.wait_ge(s_drain, jobs + (j - 1))

                def qk(s):
                    if s == 0:
                        pe.wait_ge(s_ml, G * 16 + 16)
                    elif s >= 2:
                        pe.wait_ge(s_ex, n + (s - 1))
                    scores(G, s, i, par)

                def pv(s):
                    if s == 0:
                        pe.wait_ge(s_v, b * NGB + NGB)
                        pe.wait_ge(s_oe, G + 1)
                    pe.wait_ge(s_lo, n + (s + 1))
                    weigh(s, par)

                def queries(k):
                    bank_free(J_Q + k)
                    if k == 0:
                        pe.wait_ge(s_As, G + 2)
                    project_queries(bank(J_Q + k), k, b + (i + 1) // NGB)

                next_par = (par + (i + 1) // NGB) % 2
                made = [0]

                def maxima(count):
                    if made[0] == 0:
                        pe.wait_ge(s_qh, G * 4 + 8)
                    for _ in range(count):
                        k = made[0]
                        bank_free(J_M + k)
                        max_scores(bank(J_M + k), k, next_par)
                        made[0] += 1

                def head(h):
                    bank_free(J_Y[h])
                    project_head(bank(J_Y[h]), h, (i + (NGB - 1)) % NGB)

                qk(0)
                qk(1)
                queries(0)
                qk(2)
                queries(1)
                pv(0)
                qk(3)
                bank_free(J_C)
                turn_context(bank(J_C), G + (NGB + 1))
                pv(1)
                maxima(2)
                for s in range(4, 11):
                    qk(s)
                    maxima(2)
                    pv(s - 2)
                    maxima(2)
                qk(11)
                maxima(2)
                pv(9)
                head(0)
                qk(12)
                head(1)
                pv(10)
                bank_free(J_T)
                turn_maxima(bank(J_T), G + 1)
                pv(11)
                head(2)
                head(3)
                pv(12)

            groups(pe, body)

            pe.wait_ge(s_oe, NG + 1)
            for h in range(GH):
                pe.wait_ge(s_drain, JOBS0 + JOBS * NG + h - 1)
                project_head(bank(h), h, NGB - 1)
            after_attention(pe)

            pe.wait_ge(s_mw, 160)
            turns = [(k, c) for k in range(3) for c in range(NP)]
            pe.transpose(side[:, 0, 0:E], rw_nat[:, :], ident[0:E, 0:E]).then_inc(s_kt, 1)
            for j, (lo, cut, hi, _, _) in enumerate(wturns):
                if j >= 2:
                    pe.wait_ge(s_kh, wturns[j - 2][3])
                    pe.wait_ge(s_kd, wturns[j - 2][4])
                for t, (k, c) in enumerate(turns[lo:hi]):
                    mm = pe.transpose(op[:, j % 2, t * P:(t + 1) * P], w_nat[:, k, c, :], ident[:, :])
                mm.then_inc(s_kt, 1)

            with pe.Fori(0, NCH // 2) as k:
                turn_tokens(k * 2 + NCH)
                for u in range(2):
                    pe.wait_ge(s_x2f, (k * 2 + (u + 1)) * 2)
                    pe.wait_ge(s_ls, k * 2 + (u + 1))
                    for t in range(4):
                        mm = pe.matmul(side[:, 0, t * E:(t + 1) * E], x2T_f[:, u, t * P:(t + 1) * P],
                                       rwT[:, :], start=True, stop=True)
                    mm.then_inc(s_lg, 1)

            for c in range(NCH):
                pe.wait_ge(s_rt, c + 1)
                if c:
                    pe.wait_ge(s_wk, c)
                for t in range(4):
                    mm = pe.transpose(side[:, 1, t * P:(t + 1) * P], w_cat[:, t, :], ident[:, :])
                mm.then_inc(s_wf, 1)
            pe.wait_ge(s_wk, NCH)

            gate_ps, up_ps, rep_ps = st[:, 0], st[:, 1], side

            with pe.Fori(0, NCH) as c:
                n = pe.snap(c * NP)
                chunk = bass.ds(c * BANK, BANK)

                def three(o, k, p):
                    pe.matmul(o, gu_hi[:, k, p, :], x2T_hi[:, chunk], start=True, stop=False)
                    pe.matmul(o, gu_hi[:, k, p, :], x2T_lo[:, chunk], start=False, stop=False)
                    return pe.matmul(o, gu_lo[:, k, p, :], x2T_hi[:, chunk], start=False, stop=True)

                def down(p):
                    pe.wait_ge(s_hd, n + (p + 1))
                    if p == 0:
                        pe.wait_ge(s_fin, c + 1)
                    for t in range(4):
                        mm = pe.matmul(op[:, 0, t * P:(t + 1) * P], hid[:, p % 3, t * P:(t + 1) * P],
                                       dT[:, p, :], start=(p == 0 and t == 0), stop=(p == NP - 1),
                                       skip_group_check=True)
                    mm.then_inc(s_dn, 1)

                for p in range(NP):
                    if p >= 2:
                        pe.wait_ge(s_si, n + (p - 1))
                    three(gate_ps[:, p % 2, :], 0, p).then_inc(s_ga, 1)
                    if p >= 2:
                        pe.wait_ge(s_hd, n + (p - 1))
                    mm = three(up_ps[:, p % 2, :], 1, p)
                    if p < NP - 1:
                        mm = pe.matmul(rep_ps[:, p % 2, :], sel[:, p, :], wT[:, chunk], start=True, stop=True)
                    mm.then_inc(s_up, 1)
                    if p >= 1:
                        down(p - 1)
                down(NP - 1)

        @block.scalar
        def _(act):
            act.sem_inc(s_xT, 1)
            act.sem_inc(s_oe, 1)
            act.sem_inc(s_ls, 1)
            act.wait_ge(s_var, 1)
            act.activation(std[:, :], var[:, :], ACT.Sqrt).then_inc(s_std, 1)
            with act.Fori(0, NCH // 2) as k:
                for u in range(2):
                    act.wait_ge(s_xt, k * 2 + (u + 2))
                    act.activation(xnT[:, bass.ds(k * (2 * BANK) + u * BANK, BANK)], st[:, u, 0, :],
                                   ACT.Copy).then_inc(s_xT, 1)

            def context_hi(where, i, par):
                act.activation(cT_hi[0:DC, par, bass.ds(i * BANK, BANK)], where[0:DC, :],
                               ACT.Copy).then_inc(s_ch, 1)

            def queries_hi(where, k, slot):
                cols = slice(k * BANK, (k + 1) * BANK)
                act.activation(qT_max[:, cols], where[0:DC, :], ACT.Copy).then_inc(s_qh, 1)
                act.activation(qT_hi[0:DC, slot, cols], where[0:DC, :], ACT.Copy).then_inc(s_qh, 1)

            act.wait_ge(s_set, 11)
            for i in range(NGB):
                act.wait_ge(s_fill, i + 1)
                context_hi(bank0(i), i, 0)
            for k in range(2):
                act.wait_ge(s_fill, J0_Q + k + 1)
                queries_hi(bank0(J0_Q + k), k, 0)
            act.preload_act_table(ACT.Exp)

            def body(G, b, i, par):
                n = act.snap(G * S)
                jobs = act.snap(G * JOBS + JOBS0)

                def exp(s):
                    m = rows(s)
                    act.wait_ge(s_qk, n + (s + 1))
                    if s >= 2:
                        act.wait_ge(s_lo, n + (s - 1))
                    act.activation(p_full[0:m, s % 2, :], both(st[0:m, s % 2]), ACT.Exp, scale=SCALE)
                    if s >= 4:
                        act.wait_ge(s_pv, n + (s - 3))
                    act.activation(p_hi[0:m, s % 4, :], both(st[0:m, s % 2]), ACT.Exp,
                                   scale=SCALE).then_inc(s_ex, 1)

                def queries(k):
                    act.wait_ge(s_fill, jobs + (J_Q + k + 1))
                    queries_hi(bank(J_Q + k), k, (i + 1) % 2)

                exp(0)
                exp(1)
                queries(0)
                exp(2)
                queries(1)
                exp(3)
                act.wait_ge(s_fill, jobs + (J_C + 1))
                context_hi(bank(J_C), i, 1 - par)
                for s in range(4, S):
                    exp(s)
                act.wait_ge(s_pv, n + S)
                act.activation(oT[:, :], both(op[0:OW]), ACT.Copy).then_inc(s_oe, 1)

            groups(act, body)

            after_attention(act)
            act.wait_ge(s_var, 2)
            act.activation(std[:, :], var[:, :], ACT.Sqrt).then_inc(s_std, 1)
            for j, (lo, cut, hi, _, _) in enumerate(wturns):
                act.wait_ge(s_kt, j + 2)
                gu = gu_hi[:, :, :, :].rearrange("p a b c -> p (a b) c")
                src = op[:, j % 2, :].rearrange("p (a b) -> p a b", b=P)
                if cut > lo:
                    act.activation(gu[:, lo:cut, :], src[:, 0:cut - lo, :], ACT.Copy).then_inc(s_kh, 1)
                if hi > cut:
                    act.activation(dT[:, cut - 2 * NP:hi - 2 * NP, :], src[:, cut - lo:hi - lo, :],
                                   ACT.Copy).then_inc(s_kh, 1)

            with act.Fori(0, NCH // 2) as k:
                for u in range(2):
                    act.wait_ge(s_xt, k * 2 + (NCH + u + 2))
                    act.wait_ge(s_lg, k * 2 + 1)
                    act.activation(x2T_f[:, u, :], st[:, u, 0, :], ACT.Copy).then_inc(s_x2f, 1)
                    act.activation(x2T_hi[:, bass.ds(k * (2 * BANK) + u * BANK, BANK)], st[:, u, 0, :],
                                   ACT.Copy).then_inc(s_x2f, 1)
                for u in range(2):
                    act.wait_ge(s_lg, k * 2 + (u + 2))
                    act.activation(score[:, bass.ds(k * 8 + u * 4, 4), :],
                                   side[:, 0, 0:4 * E].rearrange("p (a b) -> p a b", b=E),
                                   ACT.Exp, scale=-1.0).then_inc(s_ls, 1)

            for c in range(NCH):
                act.wait_ge(s_wf, c + 1)
                act.activation(wT[:, c * BANK:(c + 1) * BANK], side[:, 1, :], ACT.Copy).then_inc(s_wk, 1)

            with act.Fori(0, NCH) as c:
                n = act.snap(c * NP)
                for p in range(NP):
                    act.wait_ge(s_ga, n + (p + 1))
                    if p >= 2:
                        act.wait_ge(s_hd, n + (p - 1))
                    act.activation(act_g[:, p % 2, :], st[:, 0, p % 2, :], ACT.Silu).then_inc(s_si, 1)

        @block.vector
        def _(dve):
            dve.sem_inc(s_fin, 1)
            steps = [0]

            def link(ins):
                steps[0] += 1
                ins.then_inc(s_link, 1)
                dve.wait_ge(s_link, steps[0])

            def layernorm_stats(base, count):
                with dve.Fori(0, T) as t:
                    dve.bn_stats(stats[:, t, :], x1[:, t + 2, :]).then_inc(s_st, 1)
                dve.wait_ge(s_st, T * count)
                me, m2e, mo, m2o = (stats[:, :, j] for j in (1, 2, 4, 5))
                link(dve.tensor_tensor(mean[:, :], me, mo, ALU.add))
                link(dve.tensor_scalar(mean[:, :], mean[:, :], 0.5, None, ALU.mult))
                link(dve.tensor_tensor(dif[:, :], me, mo, ALU.subtract))
                link(dve.tensor_tensor(dif[:, :], dif[:, :], dif[:, :], ALU.mult))
                link(dve.tensor_tensor(var[:, :], m2e, m2o, ALU.add))
                link(dve.tensor_scalar(var[:, :], var[:, :], 1.0 / D, EPS, ALU.mult, ALU.add))
                dve.scalar_tensor_tensor(var[:, :], dif[:, :], 0.25, var[:, :], ALU.mult,
                                         ALU.add).then_inc(s_var, 1)
                dve.wait_ge(s_std, count)
                link(dve.reciprocal(rstd[:, :], std[:, :]))

            def normalise(k, u, base):
                dve.wait_ge(s_xt, k * 2 + (base + 1))
                for t in range(4):
                    tile = k * 8 + (u * 4 + t)
                    ins = dve.tensor_scalar(xn[:, u, t, :], x1[:, tile + 2, :], mean[:, bass.ds(tile, 1)],
                                            rstd[:, bass.ds(tile, 1)], ALU.subtract, ALU.mult)
                ins.then_inc(s_xn, 1)

            for k, (ap, value) in enumerate((
                    (nat[:, :, :, :], 0.0), (B_all[DC:OW, :, :], 0.0), (cT_hi[DC:OW, :, :].bitcast(F32), 1.0),
                    (v_hi[:, :, :, DC:OW].bitcast(F32), 1.0), (v_lo[:, :, :, DC:OW].bitcast(F32), 0.0),
                    (xnT[:, B * NQ:(B + 1) * NQ], 0.0), (oT[0:DC, :], 0.0), (oT[DC:OW, :], 1.0),
                    (x1[:, 0:2, :], 0.0), (B_all[0:DC, :, D:YW], 0.0))):
                dve.memset(ap, value).then_inc(s_set, 1)
            dve.wait_ge(s_set, 2)
            dve.memset(B_all[DC:OW, :, D:YW], 1.0).then_inc(s_set, 1)

            dve.wait_ge(s_x, 16)
            layernorm_stats(0, 1)
            with dve.Fori(0, NCH // 2) as k:
                for u in range(2):
                    normalise(k, u, 0)
            dve.wait_ge(s_w, 80)
            dve.wait_ge(s_xn, NCH)
            link(dve.tensor_tensor(x1[:, 2:T + 2, :], x1[:, 2:T + 2, :],
                                   bo_rows[:, :].rearrange("p (a d) -> p a d", a=1).to_broadcast([P, T, D]), ALU.add))

            for c in range(H // 2):
                dve.wait_ge(s_wt, c + 1)
                dve.tensor_copy(WT[:, 0, :], side[:, 0, 0:P])
                dve.tensor_copy(WT[:, 1, 0:DC], side[:, 0, P:P + DC])
                dve.tensor_copy(WT[:, 2, 0:DC], side[:, 0, 2 * P:2 * P + DC]).then_inc(s_wT, 1)
                if c == 0:
                    dve.wait_ge(s_set, 11)
                dve.wait_ge(s_ab, c + 1)
                for j in range(2):
                    dve.tensor_copy(A_all[:, 2 * c + j, :], a_ps[j][:, 0:DC])
                    ins = dve.tensor_copy(B_all[0:DC, 2 * c + j, 0:D], b_ps[j][0:DC, 0:P])
                ins.then_inc(s_abk, 1)

            def context_lo(where, count, i, par):
                dve.wait_ge(s_ch, count)
                cols = bass.ds(i * BANK, BANK)
                dve.tensor_tensor(cT_lo[:, par, cols], where[0:DC, :],
                                  cT_hi[0:DC, par, cols].bitcast(F32), ALU.subtract).then_inc(s_drain, 1)

            def queries_lo(where, count, k, slot):
                dve.wait_ge(s_qh, count)
                cols = slice(k * BANK, (k + 1) * BANK)
                dve.tensor_tensor(qT_lo[:, slot, cols], where[0:DC, :],
                                  qT_max[:, cols].bitcast(F32), ALU.subtract).then_inc(s_drain, 1)

            def reduce_max(where, filled, k):
                dve.wait_ge(s_fill, filled)
                dve.tensor_reduce(m_part[:, k:k + 1], where[:, 0:MAXW], AX.X, ALU.max).then_inc(s_drain, 1)

            def combine_max(reduced):
                dve.wait_ge(s_drain, reduced)
                dve.tensor_reduce(m_neg[:, :], m_part[:, :].rearrange("p (a b) -> p a b", b=4), AX.X,
                                  ALU.max, negate=True).then_inc(s_mc, 1)

            def keep_max_rows(where, filled):
                dve.wait_ge(s_fill, filled)
                dve.tensor_copy(m_row[:, :], where[0:NM // 4, 0:P]).then_inc(s_drain, 1)

            def add_head(where, filled, count, batch1):
                dve.wait_ge(s_fill, filled)
                ys = where[:, 0:2 * YW].rearrange("p (q y) -> p q y", q=2)
                dve.reciprocal(recip[:, :].rearrange("p (q y) -> p q y", q=2), ys[:, :, D:YW]).then_inc(s_rc, 1)
                dve.wait_ge(s_rc, count)
                for q in range(2):
                    tile = batch1 * 2 + q
                    ins = dve.scalar_tensor_tensor(x1[:, tile, :], ys[:, q, 0:D], recip[:, q:q + 1],
                                                   x1[:, tile, :], ALU.mult, ALU.add)
                ins.then_inc(s_drain, 1)

            for i in range(NGB):
                context_lo(bank0(i), i + 1, i, 0)
            for k in range(2):
                queries_lo(bank0(J0_Q + k), 2 * k + 2, k, 0)
            for k in range(NM):
                reduce_max(bank0(J0_M + k), J0_M + k + 1, k)
            combine_max(J0_M + NM)
            keep_max_rows(bank0(J0_T), J0_T + 1)

            def body(G, b, i, par):
                n = dve.snap(G * S)
                jobs = dve.snap(G * JOBS + JOBS0)
                batch1 = b + (i + (NGB - 1)) // NGB

                def lo(s):
                    m = rows(s)
                    dve.wait_ge(s_ex, n + (s + 1))
                    dve.tensor_tensor(p_lo[0:m, s % 4, :], p_full[0:m, s % 2, :],
                                      p_hi[0:m, s % 4, :].bitcast(F32), ALU.subtract).then_inc(s_lo, 1)

                made = [0]

                def maxima(count):
                    for _ in range(count):
                        k = made[0]
                        reduce_max(bank(J_M + k), jobs + (J_M + k + 1), k)
                        made[0] += 1

                def head(h):
                    dve.wait_ge(s_drain, jobs + J_Y[h])
                    add_head(bank(J_Y[h]), jobs + (J_Y[h] + 1), G * GH + (h + 1), batch1)

                lo(0)
                lo(1)
                queries_lo(bank(J_Q), G * 4 + 6, 0, (i + 1) % 2)
                lo(2)
                queries_lo(bank(J_Q + 1), G * 4 + 8, 1, (i + 1) % 2)
                context_lo(bank(J_C), G + (NGB + 1), i, 1 - par)
                maxima(2)
                for s in range(4, 11):
                    lo(s - 1)
                    maxima(4)
                lo(10)
                maxima(2)
                combine_max(jobs + (J_M + NM))
                head(0)
                head(1)
                lo(11)
                dve.wait_ge(s_ml, G * 16 + 16)
                keep_max_rows(bank(J_T), jobs + (J_T + 1))
                lo(12)
                head(2)
                head(3)

            groups(dve, body)
            for h in range(GH):
                dve.wait_ge(s_drain, JOBS0 + JOBS * NG + h)
                add_head(bank(h), JOBS0 + JOBS * NG + h + 1, NG * GH + h + 1, B)

            after_attention(dve)
            layernorm_stats(1, 2)
            dve.wait_ge(s_kt, 1)
            dve.tensor_copy(rwT[:, :], side[:, 0, 0:E]).then_inc(s_kd, 1)
            fh = gu_hi[:, :, :, :].rearrange("p a b c -> p (a b) c")
            fl = gu_lo[:, :, :, :].rearrange("p a b c -> p (a b) c")
            for j, (lo, cut, hi, kept, _) in enumerate(wturns):
                if cut > lo:
                    dve.wait_ge(s_kh, kept)
                    src = op[:, j % 2, :].rearrange("p (a b) -> p a b", b=P)
                    dve.tensor_tensor(fl[:, lo:cut, :], src[:, 0:cut - lo, :],
                                      fh[:, lo:cut, :].bitcast(F32), ALU.subtract).then_inc(s_kd, 1)
            with dve.Fori(0, NCH // 2) as k:
                for u in range(2):
                    normalise(k, u, NCH)
                for u in range(2):
                    dve.wait_ge(s_x2f, (k * 2 + (u + 1)) * 2)
                    cols = bass.ds(k * (2 * BANK) + u * BANK, BANK)
                    dve.tensor_tensor(x2T_lo[:, cols], st[:, u, 0, :], x2T_hi[:, cols].bitcast(F32),
                                      ALU.subtract).then_inc(s_xT, 1)

            dve.wait_ge(s_ls, NCH + 1)
            dve.wait_ge(s_mp, 3)
            by_group = lambda t: t.rearrange("p t (g e) -> p (t g) e", g=N_EGROUP)
            flat = lambda t: t.rearrange("p t g -> p (t g)")
            wide = lambda t, e: flat(t).rearrange("p (a b) -> p a b", b=1).to_broadcast([P, T * N_EGROUP, e])
            tok = lambda t: t.rearrange("p (a b) -> p a b", b=1).to_broadcast([P, T, E])
            exp = lambda t: t.rearrange("p (a b) -> p a b", a=1).to_broadcast([P, T, E])
            EG = E // N_EGROUP
            link(dve.tensor_scalar(ra[:, :, :], score[:, :, :], 1.0, None, ALU.add))
            link(dve.reciprocal(score[:, :, :], ra[:, :, :]))
            link(dve.tensor_tensor(sfc[:, :, :], score[:, :, :], exp(rb_rows[:, :]), ALU.add))
            link(dve.tensor_reduce(flat(g1[:, :, :]), by_group(sfc[:, :, :]), AX.X, ALU.max))
            link(dve.tensor_tensor(by_group(ra[:, :, :]), by_group(sfc[:, :, :]), wide(g1[:, :, :], EG), ALU.is_equal))
            link(dve.tensor_reduce(flat(g3[:, :, :]), by_group(ra[:, :, :]), AX.X, ALU.add))
            link(dve.scalar_tensor_tensor(rb[:, :, :], ra[:, :, :], -BIG, sfc[:, :, :], ALU.mult, ALU.add))
            link(dve.tensor_reduce(flat(g2[:, :, :]), by_group(rb[:, :, :]), AX.X, ALU.max))
            link(dve.tensor_scalar(g3[:, :, :], g3[:, :, :], 1.5, None, ALU.is_gt))
            link(dve.scalar_tensor_tensor(gr[:, :, :], g3[:, :, :], -BIG * 2, g2[:, :, :], ALU.mult, ALU.add))
            link(dve.tensor_scalar(g3[:, :, :], g3[:, :, :], -1.0, BIG * 2, ALU.add, ALU.mult))
            link(dve.tensor_tensor(g3[:, :, :], g3[:, :, :], g1[:, :, :], ALU.add))
            link(dve.tensor_tensor(g2[:, :, :], g3[:, :, :], gr[:, :, :], ALU.max))
            link(dve.tensor_tensor(g1[:, :, :], g1[:, :, :], g2[:, :, :], ALU.add))
            link(dve.memset(gr[:, :, :], 0.0))
            for a in range(N_EGROUP):
                for b in range(a + 1, N_EGROUP):
                    link(dve.tensor_tensor(r1[:, :], g1[:, :, a], g1[:, :, b], ALU.is_ge))
                    link(dve.tensor_tensor(gr[:, :, b], gr[:, :, b], r1[:, :], ALU.add))
                    link(dve.tensor_scalar(r1[:, :], r1[:, :], -1.0, 1.0, ALU.mult, ALU.add))
                    link(dve.tensor_tensor(gr[:, :, a], gr[:, :, a], r1[:, :], ALU.add))
            link(dve.tensor_scalar(gr[:, :, :], gr[:, :, :], TOPK_EGROUP - 0.5, None, ALU.is_lt))
            link(dve.tensor_tensor(by_group(sfc[:, :, :]), by_group(sfc[:, :, :]), wide(gr[:, :, :], EG), ALU.mult))
            link(dve.memset(rc[:, :, :], 0.0))
            for _ in range(TOP_K):
                link(dve.tensor_reduce(r1[:, :], sfc[:, :, :], AX.X, ALU.max))
                link(dve.tensor_tensor(ra[:, :, :], sfc[:, :, :], tok(r1[:, :]), ALU.is_equal))
                link(dve.tensor_tensor(ra[:, :, :], ra[:, :, :], exp(turn[:, :]), ALU.mult))
                link(dve.tensor_reduce(r1[:, :], ra[:, :, :], AX.X, ALU.max))
                link(dve.tensor_tensor(ra[:, :, :], ra[:, :, :], tok(r1[:, :]), ALU.is_equal))
                link(dve.tensor_tensor(rc[:, :, :], rc[:, :, :], ra[:, :, :], ALU.add))
                link(dve.scalar_tensor_tensor(sfc[:, :, :], ra[:, :, :], -BIG, sfc[:, :, :], ALU.mult, ALU.add))
            link(dve.tensor_tensor(ra[:, :, :], score[:, :, :], rc[:, :, :], ALU.mult))
            link(dve.tensor_reduce(r1[:, :], ra[:, :, :], AX.X, ALU.add))
            link(dve.tensor_scalar(r1[:, :], r1[:, :], 1e-20, None, ALU.add))
            link(dve.reciprocal(r1[:, :], r1[:, :]))
            link(dve.tensor_tensor(ra[:, :, :], ra[:, :, :], tok(r1[:, :]), ALU.mult))
            link(dve.tensor_scalar(ra[:, :, :], ra[:, :, :], ROUTE_SCALE, None, ALU.mult))
            link(dve.tensor_copy(w_r[:, :, :], ra[:, :, :]))
            link(dve.tensor_tensor(rb[:, :, :], ra[:, :, :], w_r[:, :, :].bitcast(F32), ALU.subtract))
            for c in range(NCH):
                if c:
                    dve.wait_ge(s_wf, c)
                tiles = slice(4 * c, 4 * c + 4)
                link(dve.tensor_copy(w_cat[:, :, 0:E], w_r[:, tiles, :].bitcast(F32)))
                dve.tensor_copy(w_cat[:, :, E:2 * E], rb[:, tiles, :]).then_inc(s_rt, 1)

            with dve.Fori(0, NCH) as c:
                n = dve.snap(c * NP)
                for p in range(NP):
                    dve.wait_ge(s_si, n + (p + 1))
                    dve.wait_ge(s_up, n + (p + 1))
                    if p >= 3:
                        dve.wait_ge(s_dn, n + (p - 2))
                    if p < NP - 1:
                        dve.tensor_tensor(gu_mul[:, p % 2, :], st[:, 1, p % 2, :], act_g[:, p % 2, :],
                                          ALU.mult).then_inc(s_gm, 1)
                        dve.wait_ge(s_gm, c * (NP - 1) + (p + 1))
                        dve.tensor_tensor(hid[:, p % 3, :], side[:, p % 2, :], gu_mul[:, p % 2, :],
                                          ALU.mult).then_inc(s_hd, 1)
                    else:
                        dve.tensor_tensor(hid[:, p % 3, :], st[:, 1, p % 2, :], act_g[:, p % 2, :],
                                          ALU.mult).then_inc(s_hd, 1)
                dve.wait_ge(s_dn, n + NP)
                tiles = bass.ds(c * 4 + 2, 4)
                dve.tensor_tensor(x1[:, tiles, :], op[:, 0, :].rearrange("p (a b) -> p a b", b=P),
                                  x1[:, tiles, :], ALU.add).then_inc(s_fin, 1)


_INS = ['x', 'ctx_768', 'L0_xattn_Wq', 'L0_xattn_Wk', 'L0_xattn_Wv', 'L0_xattn_Wo', 'L0_xattn_bo',
        'L0_ffn_router_weight', 'L0_ffn_router_bias', 'L0_ffn_gate_w', 'L0_ffn_up_w', 'L0_ffn_down_w',
        'L0_ffn_shared_gate_w', 'L0_ffn_shared_up_w', 'L0_ffn_shared_down_w']


def kernel(**inputs):
    import numpy as np
    import concourse.bacc as bacc
    from concourse.bass_utils import run_bass_kernel_spmd

    nc = bacc.Bacc("TRN2", target_bir_lowering=False, num_devices=1)
    arrays, args = {}, []
    for name in _INS:
        a = np.ascontiguousarray(inputs[name])
        arrays[f"in_{name}"] = a
        args.append(nc.dram_tensor(f"in_{name}", a.shape, mybir.dt.from_np(a.dtype), kind="ExternalInput").ap())
    out = nc.dram_tensor("out_x", inputs["x"].shape, F32, kind="ExternalOutput").ap()
    xattn_moe(nc, *args, out)
    r = run_bass_kernel_spmd(nc, [arrays], core_ids=[0])
    return r.results[0]["out_x"]
```

```python
from contextlib import ExitStack

import concourse.bass as bass
from concourse import mybir

ALU = mybir.AluOpType
ACT = mybir.ActivationFunctionType
AX = mybir.AxisListType
F32 = mybir.dt.float32
F32R = mybir.dt.float32r
I32 = mybir.dt.int32

P = 128
BANK = 512
TOP_K, N_EGROUP, TOPK_EGROUP, ROUTE_SCALE = 4, 4, 2, 2.5
EPS = 1e-5
BIG = 1e30


def xattn_moe(nc, x, ctx, Wq, Wk, Wv, Wo, bo, router_w, router_b, gate_w, up_w, down_w,
              sh_gate_w, sh_up_w, sh_down_w, out):
    B, NQ, D = x.shape
    _, NC, DC = ctx.shape
    INNER = Wq.shape[1]
    DH = 64
    H = INNER // DH
    E, EI, _ = gate_w.shape
    SCALE = float(DH) ** -0.5
    assert D == P and NQ == 2 * P and H == 16 and EI * 2 == P and sh_gate_w.shape[0] == P

    GH = 4
    GQ = GH * NQ
    NGB = H // GH
    NG = B * NGB
    FULL = NC // P
    TAIL = NC - FULL * P
    S = FULL + 1
    QT = 4
    SPAD = NGB * QT
    MAXW = 402
    DOUBLES = 4 * MAXW - NC
    NM = 4 * (GQ // P)
    T = B * NQ // P
    NCH = T // 4
    NP = E // 2 + 1
    YW = D + 1
    OW = DC + 1

    stack = ExitStack()
    with stack:
        def sb(where, name, shape, dt=F32):
            return where.enter_context(nc.sbuf_tensor(name, shape, dt))

        def sem(name):
            return stack.enter_context(nc.semaphore(name))

        x1 = sb(stack, "x1", [P, T + 2, D])
        ident = sb(stack, "ident", [P, P])
        bo_rows = sb(stack, "bo_rows", [P, D])
        stats = sb(stack, "stats", [P, T, 6])
        mean = sb(stack, "mean", [P, T])
        dif = sb(stack, "dif", [P, T])
        var = sb(stack, "var", [P, T])
        std = sb(stack, "std", [P, T])
        rstd = sb(stack, "rstd", [P, T])
        xn = sb(stack, "xn", [P, 2, 4, D])
        recip = sb(stack, "recip", [P, 2])

        att = ExitStack()
        xnT = sb(att, "xnT", [P, (B + 1) * NQ])
        A_all = sb(att, "A_all", [P, H, DC])
        B_all = sb(att, "B_all", [OW, H, YW])
        A_hi = sb(att, "A_hi", [P, GH, DC], F32R)
        A_lo = sb(att, "A_lo", [P, GH, DC], F32R)
        x_hi = sb(att, "x_hi", [P, NQ], F32R)
        x_lo = sb(att, "x_lo", [P, NQ], F32R)
        pool_spare = sb(att, "pool_spare", [P, 1])
        nat = sb(att, "nat", [P, 2, SPAD, DC])
        c_stage = sb(att, "c_stage", [P, QT, DC])
        cT_hi = sb(att, "cT_hi", [OW, 2, SPAD * P], F32R)
        cT_lo = sb(att, "cT_lo", [DC, 2, SPAD * P], F32R)
        v_hi = sb(att, "v_hi", [P, 2, SPAD, OW], F32R)
        v_lo = sb(att, "v_lo", [P, 2, SPAD, OW], F32R)
        qT_hi = sb(att, "qT_hi", [OW, 2, GQ], F32R)
        qT_lo = sb(att, "qT_lo", [DC, 2, GQ], F32R)
        qT_max = sb(att, "qT_max", [DC, GQ], F32R)
        m_part = sb(att, "m_part", [P, NM])
        m_neg = sb(att, "m_neg", [P, NM // 4])
        m_row = sb(att, "m_row", [NM // 4, P], F32R)
        oT = sb(att, "oT", [OW, GQ])
        with ExitStack() as early:
            Wq_sb = sb(early, "Wq_sb", [P, INNER])
            Wk_sb = sb(early, "Wk_sb", [DC, INNER])
            Wv_sb = sb(early, "Wv_sb", [DC, INNER])
            Wo_sb = sb(early, "Wo_sb", [P, INNER // P, D])
            WT = sb(early, "WT", [P, 2, 3, P])
        p_full = sb(att, "p_full", [P, 2, GQ])
        p_hi = sb(att, "p_hi", [P, 4, GQ], F32R)
        p_lo = sb(att, "p_lo", [P, 4, GQ], F32R)
        att.close()

        moe = stack.enter_context(ExitStack())
        x2T_hi = sb(moe, "x2T_hi", [P, T * P], F32R)
        x2T_lo = sb(moe, "x2T_lo", [P, T * P], F32R)
        x2T_f = sb(moe, "x2T_f", [P, 2, BANK])
        w_nat = sb(moe, "w_nat", [P, 3, NP, P])
        gu_hi = sb(moe, "gu_hi", [P, 2, NP, P], F32R)
        gu_lo = sb(moe, "gu_lo", [P, 2, NP, P], F32R)
        d_hi = sb(moe, "d_hi", [P, NP, P], F32R)
        d_lo = sb(moe, "d_lo", [P, NP, P], F32R)
        rw_nat = sb(moe, "rw_nat", [E, D])
        rwT = sb(moe, "rwT", [P, E])
        rb_rows = sb(moe, "rb_rows", [P, E])
        before = sb(moe, "before", [P, N_EGROUP, N_EGROUP])
        sel_plain = sb(moe, "sel_plain", [P, E // 2, P])
        sel = sb(moe, "sel", [P, E // 2, P], F32R)
        score = sb(moe, "score", [P, T + 4, E])
        choice = sb(moe, "choice", [P, 4, E + TOP_K])
        struck = sb(moe, "struck", [P, 4, E + TOP_K])
        top8 = sb(moe, "top8", [P, 4 * N_EGROUP, 8])
        best8 = sb(moe, "best8", [P, 4, 8])
        g_sum = sb(moe, "g_sum", [P, 4, N_EGROUP])
        g_more = sb(moe, "g_more", [P, 4, N_EGROUP, N_EGROUP])
        g_same = sb(moe, "g_same", [P, 4, N_EGROUP, N_EGROUP])
        g_keep = sb(moe, "g_keep", [P, 4, N_EGROUP])
        ra = sb(moe, "ra", [P, 4, E])
        sigmoid = sb(moe, "sigmoid", [P, 4, E])
        spare = sb(moe, "spare", [P, 1])
        r1 = sb(moe, "r1", [P, 4])
        w_cat = sb(moe, "w_cat", [P, 4, P])
        w_r = sb(moe, "w_r", [P, 4, E], F32R)
        wT = sb(moe, "wT", [P, T * P], F32R)
        act_g = sb(moe, "act_g", [P, 2, BANK])
        gu_mul = sb(moe, "gu_mul", [P, 2, BANK])
        hid = sb(moe, "hid", [P, 3, BANK])
        h_hi = sb(moe, "h_hi", [P, 3, BANK], F32R)
        h_lo = sb(moe, "h_lo", [P, 3, BANK], F32R)
        yT = sb(moe, "yT", [P, BANK])

        st = stack.enter_context(nc.psum_tensor("st", [P, 2, 2, BANK], F32))
        op = stack.enter_context(nc.psum_tensor("op", [P, 2, BANK], F32))
        side = stack.enter_context(nc.psum_tensor("side", [P, 2, BANK], F32))

        s_x = sem("x_landed")
        s_w = sem("attn_weights_landed")
        s_nat = [sem("context_landed_even"), sem("context_landed_odd")]
        s_id = sem("identity_ready")
        s_set = sem("padding_preset")
        s_pset = sem("constants_preset")
        s_link = sem("vector_step_done")
        s_plink = sem("pool_step_done")
        s_var = sem("variances_ready")
        s_std = sem("deviations_ready")
        s_xn = sem("tokens_normalised")
        s_xt = sem("tokens_turned")
        s_xT = sem("turned_tokens_kept")
        s_wt = sem("weights_turned")
        s_wT = sem("turned_weights_kept")
        s_ab = sem("weight_products_made")
        s_abk = sem("weight_products_kept")
        s_Ah = sem("A_and_x_hi_staged")
        s_As = sem("A_and_x_staged")
        s_cs = sem("context_staged")
        s_fill = sem("side_job_made")
        s_drain = sem("side_job_used")
        s_ch = sem("context_hi_kept")
        s_v = sem("values_split")
        s_qh = sem("queries_hi_kept")
        s_mc = sem("maxima_combined")
        s_ml = sem("maxima_row_landed")
        s_qk = sem("scores_made")
        s_ex = sem("probabilities_made")
        s_lo = sem("probabilities_lo_kept")
        s_lo_pool = sem("probabilities_lo_kept_by_pool")
        s_pv = sem("output_accumulated")
        s_oe = sem("output_kept")
        s_mr = sem("router_landed")
        s_mw = sem("moe_weights_landed")
        s_mp = sem("moe_constants_ready")
        s_kt = sem("moe_weights_turned")
        s_kh = sem("moe_weights_hi_kept")
        s_kd = sem("moe_weights_kept")
        s_lg = sem("router_logits_made")
        s_ls = sem("router_exponentials_kept")
        s_x2f = sem("x2_plain_and_hi_kept")
        s_vh = sem("values_hi_kept")
        s_st = sem("statistics_ready")
        s_bo = sem("output_bias_added")
        s_sel = sem("selectors_ready")
        s_rc = sem("heads_added_step")
        s_gm = sem("gate_times_up_made")
        s_rt = sem("routing_weights_made")
        s_wf = sem("routing_weights_turned")
        s_wk = sem("turned_routing_weights_kept")
        s_ga = sem("gate_made")
        s_up = sem("up_and_weights_made")
        s_si = sem("gate_activated")
        s_hd = sem("hidden_made")
        s_hh = sem("hidden_hi_kept")
        s_hl = sem("hidden_lo_kept")
        s_dn = sem("hidden_projected")
        s_yk = sem("turned_output_kept")
        s_yt = sem("output_turned_back")
        s_fin = sem("chunk_finished")
        s_out = sem("chunk_stored")

        x_tok = x.rearrange("b (q p) d -> p (b q) d", p=P)
        out_tok = out.rearrange("b (q p) d -> p (b q) d", p=P)
        both = lambda t: t.rearrange("p a b -> p (a b)")

        SLOTS = {2: ("MM", "M"), 3: ("MM", "M"), 4: ("MM", "MM"), 5: ("MM", "MC"), 6: ("MM", "MM"),
                 7: ("MM", "MM"), 8: ("MM", "MY"), 9: ("MM", "MM"), 10: ("MM", "MM"), 11: ("YY", "YT"),
                 12: ("", "QQ")}
        order = "".join(a + b for a, b in SLOTS.values())
        job_at = {kind: [j for j, o in enumerate(order) if o == kind] for kind in "MCYTQ"}
        assert len(job_at["M"]) == NM
        J_Q, J_C, J_M, J_T, J_Y = job_at["Q"], job_at["C"][0], job_at["M"], job_at["T"][0], job_at["Y"]
        JOBS = len(order)
        J0_Q, J0_M, J0_T, J0_Q1 = NGB, NGB + 2, NGB + 2 + NM, NGB + 3 + NM
        JOBS0 = J0_Q1 + 2
        assert JOBS % 2 == 0

        def bank0(j):
            return side[:, j % 2, :]

        def bank(j):
            return side[:, (JOBS0 + j) % 2, :]

        ab_ps = ((side[:, 1, :], op[:, 1, :]), (op[:, 0, :], st[:, 0, 1, :]))
        max_ps = (side[:, 0, :], side[:, 1, :], op[:, 0, :], op[:, 1, :])
        w_banks = (op[:, 0, :], op[:, 1, :], side[:, 1, :])
        turned = (side[:, 0, :], st[:, 1, 0, :])

        def rows(s):
            return P if s < FULL else TAIL

        POOL_STEPS = (3, 5, 7, 9)
        DVE_STEPS = tuple(s for s in range(S) if s not in POOL_STEPS)

        def wait_rest(eng, G, s):
            mine, sem = (POOL_STEPS, s_lo_pool) if s in POOL_STEPS else (DVE_STEPS, s_lo)
            eng.wait_ge(sem, G * len(mine) + (mine.index(s) + 2))

        def split_rest(eng, s):
            m = rows(s)
            eng.tensor_tensor(p_lo[0:m, slot(s), :], p_full[0:m, s % 2, :],
                              p_hi[0:m, slot(s), :].bitcast(F32),
                              ALU.subtract).then_inc(s_lo_pool if s in POOL_STEPS else s_lo, 1)

        def slot(s):
            return s % 3 if s < S - 1 else 3

        def groups(eng, body, before=None, peel=0):
            with eng.Fori(0, B // 2) as bb:
                for par in range(2):
                    if before:
                        before(eng.snap(bb * 2 + par), bb, par)
                    with eng.Fori(0, NGB - peel) as i:
                        body(eng.snap(bb * (2 * NGB) + (par * NGB) + i), bb * 2 + par, i, par)
                    for i in range(NGB - peel, NGB):
                        body(eng.snap(bb * (2 * NGB) + (par * NGB + i)), bb * 2 + par, i, par)

        wturns = [(lo, min(lo + 4, 3 * NP)) for lo in range(0, 3 * NP, 4)]

        def pieces(lo, hi, gate_up, down):
            cut = min(max(2 * NP, lo), hi)
            if cut > lo:
                yield gate_up[:, :, :, :].rearrange("p a b c -> p (a b) c")[:, lo:cut, :], slice(0, cut - lo)
            if hi > cut:
                yield down[:, cut - 2 * NP:hi - 2 * NP, :], slice(cut - lo, hi - lo)

        def pieces_kept(j):
            return sum(1 if lo >= 2 * NP or hi <= 2 * NP else 2 for lo, hi in wturns[:j + 1])

        def chunks(eng, body):
            body(0, 0, True)
            with eng.Fori(1, NCH) as c:
                body(c, eng.snap(c * NP), False)

        def after_attention(eng):
            eng.wait_ge(s_drain, JOBS0 + JOBS * NG + GH)
            eng.wait_ge(s_v, NG + NGB)
            eng.wait_ge(s_As, NG + 2)
            eng.wait_ge(s_ml, 16 * NG + 16)
            for par in range(2):
                eng.wait_ge(s_nat[par], 48 * (B // 2 + 1))

        block = stack.enter_context(nc.Block())

        @block.sync
        def _(sp):
            sp.dma_start(x1[:, 2:T + 2, :], x_tok).then_inc(s_x, 16)

            def load_context(batch, par):
                src = ctx[batch, 0:FULL * P, :].rearrange("(p t) d -> p t d", t=FULL)
                sp.dma_start(nat[:, par, 0:FULL, :], src).then_inc(s_nat[par], 16)
                sp.dma_start(nat[0:TAIL, par, FULL, :], ctx[batch, FULL * P:NC, :]).then_inc(s_nat[par], 16)
                sp.dma_start(nat[TAIL:TAIL + DOUBLES, par, FULL, :],
                             ctx[batch, 0:DOUBLES, :]).then_inc(s_nat[par], 16)

            sp.wait_ge(s_set, 1)
            load_context(0, 0)
            sp.dma_start(Wq_sb[:, :], Wq).then_inc(s_w, 16)
            sp.dma_start(Wk_sb[:, :], Wk).then_inc(s_w, 16)
            sp.dma_start(Wv_sb[:, :], Wv).then_inc(s_w, 16)
            sp.dma_start(Wo_sb[:, :, :], Wo.rearrange("(c p) n -> p c n", p=P)).then_inc(s_w, 16)
            sp.dma_start(bo_rows[:, :], bo.rearrange("(a d) -> a d", a=1).to_broadcast([P, D])).then_inc(s_w, 16)
            load_context(1, 1)

            def send_max_row(used, slot):
                sp.wait_ge(s_drain, used)
                sp.dma_start(qT_hi[DC:OW, slot, :].bitcast(F32).rearrange("o (a b) -> o a b", b=P),
                             m_row[:, :].bitcast(F32)).then_inc(s_ml, 16)

            send_max_row(J0_T + 1, 0)

            def before(b, bb, par):
                sp.wait_ge(s_v, b * NGB + NGB)
                sp.wait_ge(s_cs, b * NGB + NGB)
                load_context((bb * 2 + (par + 2)) % B, par)

            def body(G, b, i, par):
                send_max_row(G * JOBS + (JOBS0 + J_T + 1), (i + 1) % 2)

            groups(sp, body, before)

            after_attention(sp)
            sp.dma_start(rw_nat[:, :], router_w).then_inc(s_mr, 16)
            sp.dma_start(rb_rows[:, :], router_b.rearrange("(a e) -> a e", a=1).to_broadcast([P, E])).then_inc(s_mr, 16)
            for k, (w, shared) in enumerate(((gate_w, sh_gate_w), (up_w, sh_up_w))):
                for two in range(2):
                    src = w.rearrange("(c t) i h -> t i c h", t=2)[two]
                    sp.dma_start(w_nat[two * EI:(two + 1) * EI, k, 0:NP - 1, :], src).then_inc(s_mw, 16)
                sp.dma_start(w_nat[:, k, NP - 1, :], shared).then_inc(s_mw, 16)
            sp.dma_start(w_nat[:, 2, 0:NP - 1, :].rearrange("p c (t i) -> p (c t) i", t=2),
                         down_w.rearrange("e h i -> h e i")).then_inc(s_mw, 16)
            sp.dma_start(w_nat[:, 2, NP - 1, :], sh_down_w).then_inc(s_mw, 16)

            with sp.Fori(0, NCH) as c:
                sp.wait_ge(s_fin, c + 2)
                sp.dma_start(out_tok[:, bass.ds(c * 4, 4), :], x1[:, bass.ds(c * 4 + 2, 4), :]).then_inc(s_out, 16)
            sp.wait_ge(s_out, 16 * NCH)

        @block.gpsimd
        def _(pool):
            steps = [0]

            def link(ins):
                steps[0] += 1
                ins.then_inc(s_plink, 1)
                pool.wait_ge(s_plink, steps[0])

            link(pool.memset(ident[:, :], 0.0))
            pool.affine_select(out=ident[:, :], in_=ident[:, :], compare_op=ALU.not_equal, fill=1.0,
                               base=0, pattern=[[-1, P]], channel_multiplier=1).then_inc(s_id, 1)
            pool.wait_ge(s_id, 1)

            for k, (ap, value) in enumerate((
                    (cT_hi[DC:OW, :, :].bitcast(F32), 1.0), (B_all[DC:OW, :, :], 0.0), (B_all[0:DC, :, D:YW], 0.0),
                    (B_all[DC:OW, :, D:YW], 1.0), (v_hi[:, :, :, DC:OW].bitcast(F32), 1.0),
                    (v_lo[:, :, :, DC:OW].bitcast(F32), 0.0), (xnT[:, B * NQ:(B + 1) * NQ], 0.0),
                    (x1[:, 0:2, :], 0.0))):
                pool.memset(ap, value).then_inc(s_pset, 1)
                pool.wait_ge(s_pset, k + 1)

            def stage_hi(g, batch):
                pool.tensor_copy(A_hi[:, :, :], A_all[:, bass.ds(g * GH, GH), :])
                pool.tensor_copy(x_hi[:, :], xnT[:, bass.ds(batch * NQ, NQ)]).then_inc(s_Ah, 1)

            def stage_lo(g, batch, count):
                pool.wait_ge(s_Ah, count)
                pool.tensor_tensor(pool_spare[:, :], ident[:, 0:1], ident[:, 1:2], ALU.add)
                pool.tensor_tensor(A_lo[:, :, :], A_all[:, bass.ds(g * GH, GH), :],
                                   A_hi[:, :, :].bitcast(F32), ALU.subtract)
                pool.tensor_tensor(x_lo[:, :], xnT[:, bass.ds(batch * NQ, NQ)],
                                   x_hi[:, :].bitcast(F32), ALU.subtract).then_inc(s_As, 1)

            def stage_context(i, par):
                pool.tensor_copy(c_stage[:, :, :], nat[:, par, bass.ds(i * QT, QT), :]).then_inc(s_cs, 1)

            def split_values(count, i, par):
                tiles = bass.ds(i * QT, QT)
                pool.tensor_copy(v_hi[:, par, tiles, 0:DC], nat[:, par, tiles, :]).then_inc(s_vh, 1)
                pool.wait_ge(s_vh, count + 1)
                pool.tensor_tensor(v_lo[:, par, tiles, 0:DC], nat[:, par, tiles, :],
                                   v_hi[:, par, tiles, 0:DC].bitcast(F32), ALU.subtract).then_inc(s_v, 1)

            pool.wait_ge(s_nat[0], 48)
            for i in range(NGB):
                if i:
                    pool.wait_ge(s_fill, i)
                stage_context(i, 0)
            for i in range(NGB):
                split_values(i, i, 0)
            pool.wait_ge(s_abk, H // 2)
            pool.wait_ge(s_xT, NCH + 4)
            stage_hi(0, 0)
            stage_lo(0, 0, 1)
            pool.wait_ge(s_w, 80)
            pool.wait_ge(s_xn, NCH)
            pool.tensor_tensor(x1[:, 2:T + 2, :], x1[:, 2:T + 2, :],
                               bo_rows[:, :].rearrange("p (a d) -> p a d", a=1).to_broadcast([P, T, D]),
                               ALU.add).then_inc(s_bo, 1)
            pool.wait_ge(s_fill, J0_Q + 2)
            stage_hi(1, 0)
            stage_lo(1, 0, 2)

            def body(G, b, i, par):
                pool.wait_ge(s_fill, G * JOBS + JOBS0)
                pool.wait_ge(s_nat[1 - par], (b // 2) * 48 + 48 * (par + 1))
                stage_context(i, 1 - par)
                pool.wait_ge(s_oe, G + 1)
                split_values(G + NGB, i, 1 - par)
                n = pool.snap(G * S)
                for s in POOL_STEPS:
                    pool.wait_ge(s_ex, n + (s + 1))
                    split_rest(pool, s)
                    if s == POOL_STEPS[0]:
                        stage_hi((i + 2) % NGB, b + (i + 2) // NGB)
                    elif s == POOL_STEPS[1]:
                        stage_lo((i + 2) % NGB, b + (i + 2) // NGB, G + 3)

            groups(pool, body)

            after_attention(pool)
            pool.memset(score[:, T:T + 4, :], 0.0).then_inc(s_mp, 1)
            pool.memset(choice[:, :, E:E + TOP_K], -BIG).then_inc(s_mp, 1)
            pool.memset(w_cat[:, :, 2 * E:P], 0.0).then_inc(s_mp, 1)
            link(pool.memset(before[:, :, :], 0.0))
            for a in range(1, N_EGROUP):
                pool.memset(before[:, a, 0:a], 1.0).then_inc(s_mp, 1)
            link(pool.memset(sel_plain[:, :, :], 0.0))
            pick = sel_plain[:, :, :].rearrange("p c (t i) -> p c t i", t=2)
            for base in (0, -E):
                link(pool.affine_select(out=pick, in_=pick, compare_op=ALU.not_equal, fill=1.0, base=base,
                                        pattern=[[-2, E // 2], [-1, 2], [0, EI]], channel_multiplier=1))
            for part in range(2):
                cols = slice(part * E // 4, (part + 1) * E // 4)
                pool.tensor_copy(sel[:, cols, :], sel_plain[:, cols, :]).then_inc(s_sel, 1)

            with pool.Fori(0, NCH) as c:
                n = pool.snap(c * NP)
                for q in range(NP):
                    pool.wait_ge(s_hh, n + (q + 1))
                    pool.tensor_tensor(h_lo[:, q % 3, :], hid[:, q % 3, :], h_hi[:, q % 3, :].bitcast(F32),
                                       ALU.subtract).then_inc(s_hl, 1)

        @block.tensor
        def _(pe):
            pe.sem_inc(s_xt, 2)
            pe.sem_inc(s_lg, 2)
            pe.sem_inc(s_pv, 1)
            pe.wait_ge(s_id, 1)

            def turn_tokens(k, u, base):
                pe.wait_ge(s_xn, k * 4 + (base + u + 1))
                pe.wait_ge(s_xT, k * 4 + (base + u + 1))
                for t in range(4):
                    mm = pe.transpose(st[:, u % 2, u // 2, t * P:(t + 1) * P], xn[:, u % 2, t, :], ident[:, :])
                mm.then_inc(s_xt, 1)

            def turn_context(where, count):
                pe.wait_ge(s_cs, count)
                for t in range(QT):
                    mm = pe.transpose(where[0:DC, t * P:(t + 1) * P], c_stage[:, t, :], ident[:, :])
                mm.then_inc(s_fill, 1)

            def bank_free0(j):
                pe.wait_ge(s_drain, j - 1)

            for i in range(NGB):
                if i >= 2:
                    bank_free0(i)
                turn_context(bank0(i), i + 1)
            pe.wait_ge(s_w, 80)
            pe.wait_ge(s_drain, NGB)
            def turn_weights(c):
                if c >= 2:
                    pe.wait_ge(s_wT, c - 1)
                cols, o = slice(c * P, (c + 1) * P), turned[c % 2]
                pe.transpose(o[:, 0:P], Wq_sb[:, cols], ident[:, :])
                pe.transpose(o[:, P:P + DC], Wk_sb[:, cols], ident[0:DC, 0:DC])
                pe.transpose(o[:, 2 * P:2 * P + DC], Wv_sb[:, cols], ident[0:DC, 0:DC]).then_inc(s_wt, 1)

            turn_weights(0)
            for c in range(H // 2):
                if c + 1 < H // 2:
                    turn_weights(c + 1)
                pe.wait_ge(s_wT, c + 1)
                if c >= 2:
                    pe.wait_ge(s_abk, c - 1)
                for j in range(2):
                    r = slice(j * DH, (j + 1) * DH)
                    pe.matmul(ab_ps[c % 2][j][:, 0:DC], WT[r, c % 2, 0, :], WT[r, c % 2, 1, 0:DC], start=True, stop=True)
                    mm = pe.matmul(ab_ps[c % 2][j][0:DC, P:2 * P], WT[r, c % 2, 2, 0:DC], Wo_sb[r, c, :], start=True, stop=True)
                mm.then_inc(s_ab, 1)
            pe.wait_ge(s_abk, H // 2)
            with pe.Fori(0, NCH // 4) as k:
                for u in range(4):
                    turn_tokens(k, u, 0)

            def project_queries(where, k):
                for h in range(2):
                    o = where[0:DC, h * NQ:(h + 1) * NQ]
                    pe.matmul(o, A_hi[:, 2 * k + h, :], x_hi[:, :], start=True, stop=False)
                    pe.matmul(o, A_hi[:, 2 * k + h, :], x_lo[:, :], start=False, stop=False)
                    mm = pe.matmul(o, A_lo[:, 2 * k + h, :], x_hi[:, :], start=False, stop=True)
                mm.then_inc(s_fill, 1)

            def max_scores(where, k, par):
                tile, part = k % (NM // 4), k // (NM // 4)
                pe.matmul(where[:, 0:MAXW], qT_max[:, tile * P:(tile + 1) * P],
                          cT_hi[0:DC, par, part * MAXW:(part + 1) * MAXW],
                          start=True, stop=True).then_inc(s_fill, 1)

            def turn_maxima(where, g):
                pe.wait_ge(s_mc, g + 1)
                pe.transpose(where[0:NM // 4, 0:P], m_neg[:, :], ident[:, :]).then_inc(s_fill, 1)

            pe.wait_ge(s_pset, 8)
            pe.wait_ge(s_xT, NCH + 4)
            pe.wait_ge(s_As, 1)
            for k in range(2):
                bank_free0(J0_Q + k)
                project_queries(bank0(J0_Q + k), k)
            pe.wait_ge(s_qh, 4)
            for k in range(NM):
                pe.wait_ge(s_drain, J0_M + max(k - 3, 0))
                max_scores(max_ps[k % 4], k, 0)
            pe.wait_ge(s_drain, J0_T)
            turn_maxima(bank0(J0_T), 0)
            pe.wait_ge(s_As, 2)
            for k in range(2):
                bank_free0(J0_Q1 + k)
                project_queries(bank0(J0_Q1 + k), k)

            def scores(s, i, par):
                m = rows(s)
                keys = slice(s * P, s * P + m)
                for j in range(2):
                    cols = slice(j * BANK, (j + 1) * BANK)
                    o = st[0:m, s % 2, j, :]
                    pe.matmul(o, cT_hi[:, par, keys], qT_hi[:, i % 2, cols], start=True, stop=False)
                    pe.matmul(o, cT_hi[0:DC, par, keys], qT_lo[:, i % 2, cols], start=False, stop=False)
                    mm = pe.matmul(o, cT_lo[:, par, keys], qT_hi[0:DC, i % 2, cols], start=False, stop=True)
                mm.then_inc(s_qk, 1)

            def weigh(s, par):
                m = rows(s)
                for j in range(2):
                    cols = slice(j * BANK, (j + 1) * BANK)
                    o = op[0:OW, j, :]
                    pe.matmul(o, v_hi[0:m, par, s, :], p_hi[0:m, slot(s), cols], start=(s == 0), stop=False)
                    pe.matmul(o, v_hi[0:m, par, s, :], p_lo[0:m, slot(s), cols], start=False, stop=False)
                    mm = pe.matmul(o, v_lo[0:m, par, s, :], p_hi[0:m, slot(s), cols], start=False,
                                   stop=(s == S - 1))
                mm.then_inc(s_pv, 1)

            def project_head(where, h, g):
                for q in range(2):
                    at = h * NQ + q * P
                    mm = pe.matmul(where[:, q * YW:(q + 1) * YW], oT[:, at:at + P],
                                   B_all[:, g * GH + h, :], start=True, stop=True)
                mm.then_inc(s_fill, 1)

            def body(G, b, i, par):
                n = pe.snap(G * S)
                jobs = pe.snap(G * JOBS + JOBS0)

                def bank_free(j):
                    pe.wait_ge(s_drain, jobs + (j - 1))

                def qk(s):
                    pe.wait_ge(s_ex, n + (s - 1))
                    scores(s, i, par)

                def pv(s):
                    if s == 0:
                        pe.wait_ge(s_v, b * NGB + NGB)
                        pe.wait_ge(s_oe, G + 1)
                    wait_rest(pe, G, s)
                    weigh(s, par)

                next_par = (par + (i + 1) // NGB) % 2
                made = dict.fromkeys("MCYTQ", 0)

                def side_jobs(kinds):
                    for kind in kinds:
                        k = made[kind]
                        j = job_at[kind][k]
                        made[kind] += 1
                        pe.wait_ge(s_drain, jobs + (j - 1))
                        if kind == "M":
                            if k == 0:
                                pe.wait_ge(s_qh, G * 4 + 8)
                            max_scores(bank(j), k, next_par)
                        elif kind == "C":
                            turn_context(bank(j), G + (NGB + 1))
                        elif kind == "Y":
                            project_head(bank(j), k, (i + (NGB - 1)) % NGB)
                        elif kind == "T":
                            turn_maxima(bank(j), G + 1)
                        else:
                            if k == 0:
                                pe.wait_ge(s_As, G + 3)
                            project_queries(bank(j), k)

                for t in range(2, S):
                    qk(t)
                    side_jobs(SLOTS[t][0])
                    pv(t - 2)
                    side_jobs(SLOTS[t][1])
                pv(S - 2)
                pe.wait_ge(s_ml, G * 16 + 32)
                pe.wait_ge(s_ex, n + S)
                scores(0, (i + 1) % 2, next_par)
                pv(S - 1)
                scores(1, (i + 1) % 2, next_par)

            pe.wait_ge(s_ml, 16)
            scores(0, 0, 0)
            scores(1, 0, 0)
            groups(pe, body, peel=1)

            pe.wait_ge(s_oe, NG + 1)
            for h in range(GH):
                pe.wait_ge(s_drain, JOBS0 + JOBS * NG + h - 1)
                project_head(bank(h), h, NGB - 1)
            after_attention(pe)

            pe.wait_ge(s_mr, 32)
            pe.transpose(side[:, 0, 0:E], rw_nat[:, :], ident[0:E, 0:E]).then_inc(s_kt, 1)
            def route_logits(k, u):
                pe.wait_ge(s_x2f, k * 8 + (2 * u + 2))
                pe.wait_ge(s_ls, k * 4 + (u + 1))
                for t in range(4):
                    mm = pe.matmul(side[:, 0, t * E:(t + 1) * E], x2T_f[:, u % 2, t * P:(t + 1) * P],
                                   rwT[:, :], start=True, stop=True)
                mm.then_inc(s_lg, 1)

            with pe.Fori(0, NCH // 4) as k:
                for u in range(4):
                    turn_tokens(k, u, NCH)
                    if u:
                        route_logits(k, u - 1)
                route_logits(k, 3)

            pe.wait_ge(s_mw, 128)
            matrices = [(k, c) for k in range(3) for c in range(NP)]
            for j, (lo, hi) in enumerate(wturns):
                if j >= 3:
                    pe.wait_ge(s_kd, pieces_kept(j - 3))
                for t, (k, c) in enumerate(matrices[lo:hi]):
                    mm = pe.transpose(w_banks[j % 3][:, t * P:(t + 1) * P], w_nat[:, k, c, :], ident[:, :])
                mm.then_inc(s_kt, 1)
            pe.wait_ge(s_kd, pieces_kept(len(wturns) - 1))
            pe.wait_ge(s_xT, 2 * NCH + 4)
            pe.wait_ge(s_ls, NCH + 1)

            gate_ps, up_ps, rep_ps = st[:, 0], st[:, 1], side

            def three(o, hi_w, lo_w, hi_x, lo_x, start=True, stop=True):
                pe.matmul(o, hi_w, hi_x, start=start, stop=False)
                pe.matmul(o, hi_w, lo_x, start=False, stop=False)
                return pe.matmul(o, lo_w, hi_x, start=False, stop=stop)

            def down(n, q):
                w = (q - 1) % NP
                pe.wait_ge(s_hl, n + (q + 1))
                three(op[:, 0, :], d_hi[:, w, :], d_lo[:, w, :], h_hi[:, q % 3, :], h_lo[:, q % 3, :],
                      start=(q == 0), stop=(q == NP - 1)).then_inc(s_dn, 1)

            def turn_output(c):
                pe.wait_ge(s_yk, c + 1)
                for t in range(4):
                    mm = pe.transpose(op[:, 1, t * P:(t + 1) * P], yT[:, t * P:(t + 1) * P], ident[:, :])
                mm.then_inc(s_yt, 1)

            def body(c, n, first):
                chunk = bass.ds(c * BANK, BANK)
                pe.wait_ge(s_rt, c + 1)
                if not first:
                    pe.wait_ge(s_fin, c)
                for t in range(4):
                    mm = pe.transpose(op[:, 1, t * P:(t + 1) * P], w_cat[:, t, :], ident[:, :])
                mm.then_inc(s_wf, 1)
                for q in range(NP):
                    w = (q - 1) % NP
                    if q >= 2:
                        pe.wait_ge(s_si, n + (q - 1))
                    elif q == 0 and not first:
                        pe.wait_ge(s_si, n)
                    three(gate_ps[:, q % 2, :], gu_hi[:, 0, w, :], gu_lo[:, 0, w, :],
                          x2T_hi[:, chunk], x2T_lo[:, chunk]).then_inc(s_ga, 1)
                    if q >= 2:
                        pe.wait_ge(s_hd, n + (q - 1))
                    elif q == 0 and not first:
                        pe.wait_ge(s_hd, n)
                    mm = three(up_ps[:, q % 2, :], gu_hi[:, 1, w, :], gu_lo[:, 1, w, :],
                               x2T_hi[:, chunk], x2T_lo[:, chunk])
                    if q:
                        if q == 1:
                            pe.wait_ge(s_wk, c + 1)
                            if first:
                                pe.wait_ge(s_sel, 2)
                        mm = pe.matmul(rep_ps[:, q % 2, :], sel[:, w, :], wT[:, chunk], start=True, stop=True)
                    mm.then_inc(s_up, 1)
                    if q >= 2:
                        if q == 2 and not first:
                            pe.wait_ge(s_yk, c)
                        down(n, q - 2)
                    elif not first:
                        down(n - NP, q - 2 + NP)
                    if q == 3 and not first:
                        turn_output(c - 1)

            chunks(pe, body)
            for q in (NP - 2, NP - 1):
                down((NCH - 1) * NP, q)
            turn_output(NCH - 1)

        @block.scalar
        def _(act):
            act.sem_inc(s_xT, 4)
            act.sem_inc(s_ls, 1)
            def context_hi(where, i, par):
                act.activation(cT_hi[0:DC, par, bass.ds(i * BANK, BANK)], where[0:DC, :],
                               ACT.Copy).then_inc(s_ch, 1)

            def queries_hi(where, k, slot):
                cols = slice(k * BANK, (k + 1) * BANK)
                act.activation(qT_max[:, cols], where[0:DC, :], ACT.Copy).then_inc(s_qh, 1)
                act.activation(qT_hi[0:DC, slot, cols], where[0:DC, :], ACT.Copy).then_inc(s_qh, 1)

            act.wait_ge(s_pset, 8)
            for i in range(NGB):
                act.wait_ge(s_fill, i + 1)
                context_hi(bank0(i), i, 0)
            def keep_turned_weights(c):
                act.wait_ge(s_wt, c + 1)
                if c >= 2:
                    act.wait_ge(s_ab, c - 1)
                o = turned[c % 2]
                act.activation(WT[:, c % 2, 0, :], o[:, 0:P], ACT.Copy)
                act.activation(WT[:, c % 2, 1:3, 0:DC], o[:, P:3 * P].rearrange("p (a b) -> p a b", b=P)[:, :, 0:DC],
                               ACT.Copy).then_inc(s_wT, 1)

            keep_turned_weights(0)
            for c in range(H // 2):
                if c + 1 < H // 2:
                    keep_turned_weights(c + 1)
                act.wait_ge(s_ab, c + 1)
                for j in range(2):
                    act.activation(A_all[:, 2 * c + j, :], ab_ps[c % 2][j][:, 0:DC], ACT.Copy)
                    ins = act.activation(B_all[0:DC, 2 * c + j, 0:D], ab_ps[c % 2][j][0:DC, P:2 * P], ACT.Copy)
                ins.then_inc(s_abk, 1)
            act.wait_ge(s_var, 1)
            act.activation(std[:, :], var[:, :], ACT.Sqrt).then_inc(s_std, 1)
            with act.Fori(0, NCH // 4) as k:
                for u in range(4):
                    act.wait_ge(s_xt, k * 4 + (u + 3))
                    act.activation(xnT[:, bass.ds(k * (4 * BANK) + u * BANK, BANK)], st[:, u % 2, u // 2, :],
                                   ACT.Copy).then_inc(s_xT, 1)
            for k in range(2):
                act.wait_ge(s_fill, J0_Q + k + 1)
                queries_hi(bank0(J0_Q + k), k, 0)
            for k in range(2):
                act.wait_ge(s_fill, J0_Q1 + k + 1)
                queries_hi(bank0(J0_Q1 + k), k, 1)
            act.wait_ge(s_set, 2)
            act.preload_act_table(ACT.Exp)

            def keep_output(steps):
                act.wait_ge(s_pv, steps + 1)
                act.activation(oT[:, :], both(op[0:OW]), ACT.Copy).then_inc(s_oe, 1)

            def body(G, b, i, par):
                n = act.snap(G * S)
                jobs = act.snap(G * JOBS + JOBS0)

                def exp(s):
                    m = rows(s)
                    act.wait_ge(s_qk, n + (s + 1))
                    if s >= 2:
                        wait_rest(act, G, s - 2)
                    elif s == 0:
                        act.wait_ge(s_lo, G * len(DVE_STEPS) + 1)
                    act.activation(p_full[0:m, s % 2, :], both(st[0:m, s % 2]), ACT.Exp, scale=SCALE)
                    if 3 <= s < S - 1:
                        act.wait_ge(s_pv, n + (s - 1))
                    act.activation(p_hi[0:m, slot(s), :], both(st[0:m, s % 2]), ACT.Exp,
                                   scale=SCALE).then_inc(s_ex, 1)

                exp(0)
                keep_output(n)
                for s in range(1, S):
                    exp(s)
                    if "C" in "".join(SLOTS.get(s + 1, ())):
                        act.wait_ge(s_fill, jobs + (J_C + 1))
                        context_hi(bank(J_C), i, 1 - par)
                for k in range(2):
                    act.wait_ge(s_fill, jobs + (J_Q[k] + 1))
                    queries_hi(bank(J_Q[k]), k, i % 2)

            groups(act, body)
            keep_output(NG * S)

            after_attention(act)
            act.wait_ge(s_var, 2)
            act.activation(std[:, :], var[:, :], ACT.Sqrt).then_inc(s_std, 1)
            act.wait_ge(s_kt, 1)
            act.activation(rwT[:, :], side[:, 0, 0:E], ACT.Copy)
            act.preload_act_table(ACT.Exp)
            def keep_exponentials(k, u):
                act.wait_ge(s_lg, k * 4 + (u + 3))
                act.activation(score[:, bass.ds(k * 16 + u * 4, 4), :],
                               side[:, 0, 0:4 * E].rearrange("p (a b) -> p a b", b=E),
                               ACT.Exp, scale=-1.0).then_inc(s_ls, 1)

            with act.Fori(0, NCH // 4) as k:
                for u in range(4):
                    act.wait_ge(s_xt, k * 4 + (NCH + u + 3))
                    act.wait_ge(s_lg, k * 4 + (u + 1))
                    where = st[:, u % 2, u // 2, :]
                    act.activation(x2T_f[:, u % 2, :], where, ACT.Copy).then_inc(s_x2f, 1)
                    act.activation(x2T_hi[:, bass.ds(k * (4 * BANK) + u * BANK, BANK)], where,
                                   ACT.Copy).then_inc(s_x2f, 1)
                    if u:
                        keep_exponentials(k, u - 1)
                keep_exponentials(k, 3)

            for j, (lo, hi) in enumerate(wturns):
                act.wait_ge(s_kt, j + 2)
                src = w_banks[j % 3].rearrange("p (a b) -> p a b", b=P)
                for place, cols in pieces(lo, hi, gu_hi, d_hi):
                    act.activation(place, src[:, cols, :], ACT.Copy).then_inc(s_kh, 1)
            act.preload_act_table(ACT.Silu)

            def hidden_hi(n, q, used):
                act.wait_ge(s_hd, n + (q + 1))
                if used is not None:
                    act.wait_ge(s_dn, used)
                act.activation(h_hi[:, q % 3, :], hid[:, q % 3, :], ACT.Copy).then_inc(s_hh, 1)

            def keep_output_T(c):
                act.wait_ge(s_dn, c * NP + NP)
                act.activation(yT[:, :], op[:, 0, :], ACT.Copy).then_inc(s_yk, 1)

            def body(c, n, first):
                act.wait_ge(s_wf, c + 1)
                act.activation(wT[:, bass.ds(c * BANK, BANK)], op[:, 1, :], ACT.Copy).then_inc(s_wk, 1)
                for q in range(NP):
                    if q == 2 and not first:
                        keep_output_T(c - 1)
                    act.wait_ge(s_ga, n + (q + 1))
                    if q >= 2:
                        act.wait_ge(s_hd, n + (q - 1))
                    elif q == 0 and not first:
                        act.wait_ge(s_hd, n)
                    act.activation(act_g[:, q % 2, :], st[:, 0, q % 2, :], ACT.Silu).then_inc(s_si, 1)
                    if q == 0:
                        if not first:
                            hidden_hi(n - NP, NP - 1, n - NP + (NP - 3))
                    elif q >= 4:
                        hidden_hi(n, q - 1, n + (q - 3))
                    else:
                        hidden_hi(n, q - 1, None if first else n + min(q - 2, 0))

            chunks(act, body)
            hidden_hi((NCH - 1) * NP, NP - 1, NCH * NP - 3)
            keep_output_T(NCH - 1)

        @block.vector
        def _(dve):
            dve.sem_inc(s_lo, 1)
            dve.sem_inc(s_lo_pool, 1)
            dve.sem_inc(s_fin, 1)
            steps = [0]
            turns = [0]

            def link(ins):
                steps[0] += 1
                ins.then_inc(s_link, 1)
                dve.wait_ge(s_link, turns[0] + steps[0])

            def tile_stats(tile):
                dve.bn_stats(stats[:, tile, :], x1[:, tile + 2, :]).then_inc(s_st, 1)

            def layernorm_stats(stats_made):
                dve.wait_ge(s_st, stats_made)
                me, m2e, mo, m2o = (stats[:, :, j] for j in (1, 2, 4, 5))
                link(dve.tensor_tensor(mean[:, :], me, mo, ALU.add))
                link(dve.tensor_scalar(mean[:, :], mean[:, :], 0.5, None, ALU.mult))
                link(dve.tensor_tensor(dif[:, :], me, mo, ALU.subtract))
                link(dve.tensor_tensor(dif[:, :], dif[:, :], dif[:, :], ALU.mult))
                link(dve.tensor_tensor(var[:, :], m2e, m2o, ALU.add))
                link(dve.tensor_scalar(var[:, :], var[:, :], 1.0 / D, EPS, ALU.mult, ALU.add))
                dve.scalar_tensor_tensor(var[:, :], dif[:, :], 0.25, var[:, :], ALU.mult,
                                         ALU.add).then_inc(s_var, 1)

            def reciprocal_deviations(count):
                dve.wait_ge(s_std, count)
                link(dve.reciprocal(rstd[:, :], std[:, :]))

            def normalise(k, u, base):
                dve.wait_ge(s_xt, k * 4 + (base + u + 1))
                for t in range(4):
                    tile = k * 16 + (u * 4 + t)
                    ins = dve.tensor_scalar(xn[:, u % 2, t, :], x1[:, tile + 2, :], mean[:, bass.ds(tile, 1)],
                                            rstd[:, bass.ds(tile, 1)], ALU.subtract, ALU.mult)
                ins.then_inc(s_xn, 1)

            dve.memset(nat[:, :, :, :], 0.0).then_inc(s_set, 1)

            def context_lo(where, count, i, par):
                dve.wait_ge(s_ch, count)
                cols = bass.ds(i * BANK, BANK)
                dve.tensor_tensor(cT_lo[:, par, cols], where[0:DC, :],
                                  cT_hi[0:DC, par, cols].bitcast(F32), ALU.subtract).then_inc(s_drain, 1)

            for i in range(NGB):
                context_lo(bank0(i), i + 1, i, 0)
            dve.wait_ge(s_x, 16)
            with dve.Fori(0, T // 8) as t:
                for u in range(8):
                    tile_stats(dve.snap(t * 8 + u))
            layernorm_stats(T)

            reciprocal_deviations(1)
            with dve.Fori(0, NCH // 4) as k:
                for u in range(4):
                    normalise(k, u, 0)

            def queries_lo(where, count, k, slot):
                dve.wait_ge(s_qh, count)
                cols = slice(k * BANK, (k + 1) * BANK)
                dve.tensor_tensor(qT_lo[:, slot, cols], where[0:DC, :],
                                  qT_max[:, cols].bitcast(F32), ALU.subtract).then_inc(s_drain, 1)

            def reduce_max(where, filled, k):
                dve.wait_ge(s_fill, filled)
                k = k % (NM // 4) * 4 + k // (NM // 4)
                dve.tensor_reduce(m_part[:, k:k + 1], where[:, 0:MAXW], AX.X, ALU.max).then_inc(s_drain, 1)

            def combine_max(reduced):
                dve.wait_ge(s_drain, reduced)
                dve.tensor_reduce(m_neg[:, :], m_part[:, :].rearrange("p (a b) -> p a b", b=4), AX.X,
                                  ALU.max, negate=True).then_inc(s_mc, 1)

            def keep_max_rows(where, filled):
                dve.wait_ge(s_fill, filled)
                dve.tensor_copy(m_row[:, :], where[0:NM // 4, 0:P]).then_inc(s_drain, 1)

            def add_head(where, filled, count, batch1):
                dve.wait_ge(s_fill, filled)
                ys = where[:, 0:2 * YW].rearrange("p (q y) -> p q y", q=2)
                dve.reciprocal(recip[:, :].rearrange("p (q y) -> p q y", q=2), ys[:, :, D:YW]).then_inc(s_rc, 1)
                dve.wait_ge(s_rc, count)
                for q in range(2):
                    tile = batch1 * 2 + q
                    ins = dve.scalar_tensor_tensor(x1[:, tile, :], ys[:, q, 0:D], recip[:, q:q + 1],
                                                   x1[:, tile, :], ALU.mult, ALU.add)
                ins.then_inc(s_drain, 1)

            for k in range(2):
                queries_lo(bank0(J0_Q + k), 2 * k + 2, k, 0)
            for k in range(NM):
                reduce_max(max_ps[k % 4], J0_M + k + 1, k)
            combine_max(J0_M + NM)
            dve.memset(op[0:OW, :, :], 1.0).then_inc(s_set, 1)
            keep_max_rows(bank0(J0_T), J0_T + 1)
            for k in range(2):
                queries_lo(bank0(J0_Q1 + k), 2 * k + 6, k, 1)

            def body(G, b, i, par):
                n = dve.snap(G * S)
                jobs = dve.snap(G * JOBS + JOBS0)
                batch1 = b + (i + (NGB - 1)) // NGB

                def lo(s):
                    if s in DVE_STEPS:
                        dve.wait_ge(s_ex, n + (s + 1))
                        split_rest(dve, s)

                made = dict.fromkeys("MCYTQ", 0)

                def side_jobs(kinds):
                    for kind in kinds:
                        k = made[kind]
                        j = job_at[kind][k]
                        made[kind] += 1
                        filled = jobs + (j + 1)
                        if kind == "M":
                            reduce_max(bank(j), filled, k)
                            if k == NM - 1:
                                combine_max(filled)
                        elif kind == "C":
                            context_lo(bank(j), G + (NGB + 1), i, 1 - par)
                        elif kind == "Y":
                            dve.wait_ge(s_drain, jobs + j)
                            add_head(bank(j), filled, G * GH + (k + 1), batch1)
                        elif kind == "T":
                            dve.wait_ge(s_ml, G * 16 + 16)
                            keep_max_rows(bank(j), filled)
                        else:
                            queries_lo(bank(j), G * 4 + (10 + 2 * k), k, i % 2)

                lo(0)
                for t in range(2, S):
                    side_jobs(SLOTS[t][0])
                    lo(t - 1)
                    if t == S - 1:
                        lo(t)
                    side_jobs(SLOTS[t][1])

            def before_batch(b, bb, par):
                for u in range(2):
                    tile_stats(dve.snap((b + (B - 2)) % B * 2 + u))

            dve.wait_ge(s_bo, 1)
            groups(dve, body, before_batch)
            for h in range(GH):
                dve.wait_ge(s_drain, JOBS0 + JOBS * NG + h)
                add_head(bank(h), JOBS0 + JOBS * NG + h + 1, NG * GH + h + 1, B)

            dve.wait_ge(s_drain, JOBS0 + JOBS * NG + GH)
            for tile in range(T - 4, T):
                tile_stats(tile)
            layernorm_stats(T + T + 4)
            after_attention(dve)
            reciprocal_deviations(2)

            def tokens_lo(k, u):
                dve.wait_ge(s_x2f, k * 8 + (2 * u + 2))
                cols = bass.ds(k * (4 * BANK) + u * BANK, BANK)
                dve.tensor_tensor(x2T_lo[:, cols], st[:, u % 2, u // 2, :], x2T_hi[:, cols].bitcast(F32),
                                  ALU.subtract).then_inc(s_xT, 1)

            with dve.Fori(0, NCH // 4) as k:
                for u in range(4):
                    normalise(k, u, NCH)
                    if u:
                        tokens_lo(k, u - 1)
                tokens_lo(k, 3)
            tok = lambda t: t.rearrange("p (a b) -> p a b", b=1).to_broadcast([P, 4, E])
            exp = lambda t: t.rearrange("p (a b) -> p a b", a=1).to_broadcast([P, 4, E])
            one = lambda t: t.rearrange("p t (g a) -> p t g a", a=1)

            def wait_here():
                dve.memset(spare[:, :], 0.0)

            def route_scores(sc):
                link(dve.tensor_scalar(ra[:, :, :], sc, 1.0, None, ALU.add))
                link(dve.reciprocal(sigmoid[:, :, :], ra[:, :, :]))
                link(dve.tensor_tensor(choice[:, :, 0:E], sigmoid[:, :, :], exp(rb_rows[:, :]), ALU.add))
                wait_here()

            def route_largest():
                for t in range(4):
                    for g in range(N_EGROUP):
                        ins = dve.max(top8[:, t * N_EGROUP + g, :],
                                      choice[:, t, g * (E // N_EGROUP):(g + 1) * (E // N_EGROUP)])
                link(ins)
                flat = g_sum[:, :, :].rearrange("p t g -> p (t g)")
                link(dve.tensor_tensor(flat, top8[:, :, 0], top8[:, :, 1], ALU.add))

            def route_groups():
                mine = one(g_sum[:, :, :]).to_broadcast([P, 4, N_EGROUP, N_EGROUP])
                other = g_sum[:, :, :].rearrange("p t (a g) -> p t a g", a=1).to_broadcast([P, 4, N_EGROUP, N_EGROUP])
                dve.tensor_tensor(g_more[:, :, :, :], other, mine, ALU.is_gt)
                link(dve.tensor_tensor(g_same[:, :, :, :], other, mine, ALU.is_equal))
                earlier = before[:, :, :].rearrange("p (t a) b -> p t a b", t=1).to_broadcast([P, 4, N_EGROUP, N_EGROUP])
                link(dve.tensor_tensor(g_same[:, :, :, :], g_same[:, :, :, :], earlier, ALU.mult))
                link(dve.tensor_tensor(g_more[:, :, :, :], g_more[:, :, :, :], g_same[:, :, :, :], ALU.add))
                link(dve.tensor_reduce(g_keep[:, :, :], g_more[:, :, :, :], AX.X, ALU.add))
                link(dve.tensor_scalar(g_keep[:, :, :], g_keep[:, :, :], TOPK_EGROUP - 0.5, None, ALU.is_lt))

            def route_experts():
                for t in range(4):
                    rows_ = choice[:, t, 0:E].rearrange("p (g e) -> p g e", g=N_EGROUP)
                    keep = g_keep[:, t, :].rearrange("p (g a) -> p g a", a=1).to_broadcast([P, N_EGROUP, E // N_EGROUP])
                    ins = dve.tensor_tensor(rows_, rows_, keep, ALU.mult)
                link(ins)
                wait_here()
                for t in range(4):
                    ins = dve.max(best8[:, t, :], choice[:, t, 0:E])
                link(ins)
                link(dve.memset(best8[:, :, TOP_K:8], -BIG))
                wait_here()
                for t in range(4):
                    ins = dve.match_replace(out=struck[:, t, :], in_to_replace=best8[:, t, :],
                                            in_values=choice[:, t, :], imm_value=BIG)
                link(ins)

            def route_weights():
                link(dve.tensor_tensor(ra[:, :, :], struck[:, :, 0:E], choice[:, :, 0:E], ALU.not_equal))
                link(dve.tensor_tensor(ra[:, :, :], sigmoid[:, :, :], ra[:, :, :], ALU.mult))
                link(dve.tensor_reduce(r1[:, :], ra[:, :, :], AX.X, ALU.add))
                link(dve.tensor_scalar(r1[:, :], r1[:, :], 1e-20, None, ALU.add))
                link(dve.reciprocal(r1[:, :], r1[:, :]))
                link(dve.scalar_tensor_tensor(ra[:, :, :], ra[:, :, :], ROUTE_SCALE, tok(r1[:, :]), ALU.mult, ALU.mult))

            def keep_weights(turned_before):
                link(dve.tensor_copy(w_r[:, :, :], ra[:, :, :]))
                if turned_before is not None:
                    dve.wait_ge(s_wf, turned_before)
                dve.tensor_copy(w_cat[:, :, 0:E], w_r[:, :, :].bitcast(F32))
                dve.tensor_tensor(w_cat[:, :, E:2 * E], ra[:, :, :], w_r[:, :, :].bitcast(F32),
                                  ALU.subtract).then_inc(s_rt, 1)

            dve.wait_ge(s_ls, NCH + 1)
            dve.wait_ge(s_mp, 2 + N_EGROUP)
            for j, (lo, hi) in enumerate(wturns):
                src = w_banks[j % 3].rearrange("p (a b) -> p a b", b=P)
                dve.wait_ge(s_kh, pieces_kept(j))
                for (hi_part, cols), (lo_part, _) in zip(pieces(lo, hi, gu_hi, d_hi), pieces(lo, hi, gu_lo, d_lo)):
                    dve.tensor_tensor(lo_part, src[:, cols, :], hi_part.bitcast(F32), ALU.subtract).then_inc(s_kd, 1)
                if j == 2:
                    route_scores(score[:, 0:4, :])
                elif j == 4:
                    route_largest()
                elif j == 6:
                    route_groups()
                elif j == 8:
                    route_experts()
                elif j == 10:
                    route_weights()
            keep_weights(None)

            def add_output(c):
                dve.wait_ge(s_yt, c + 1)
                tiles = bass.ds(c * 4 + 2, 4)
                dve.tensor_tensor(x1[:, tiles, :], op[:, 1, :].rearrange("p (a b) -> p a b", b=P),
                                  x1[:, tiles, :], ALU.add).then_inc(s_fin, 1)

            def body(c, n, first):
                start = steps[0]
                if not first:
                    turns[0] = dve.snap((c - 1) * per_chunk[0])
                sc = score[:, bass.ds(c * 4 + 4, 4), :]
                for q in range(NP):
                    dve.wait_ge(s_si, n + (q + 1))
                    dve.wait_ge(s_up, n + (q + 1))
                    if q >= 3:
                        dve.wait_ge(s_hl, n + (q - 2))
                    elif not first:
                        dve.wait_ge(s_hl, n + min(q - 1, 0))
                    if q:
                        dve.tensor_tensor(gu_mul[:, q % 2, :], st[:, 1, q % 2, :], act_g[:, q % 2, :],
                                          ALU.mult).then_inc(s_gm, 1)
                        dve.wait_ge(s_gm, c * (NP - 1) + q)
                        dve.tensor_tensor(hid[:, q % 3, :], side[:, q % 2, :], gu_mul[:, q % 2, :],
                                          ALU.mult).then_inc(s_hd, 1)
                    else:
                        dve.tensor_tensor(hid[:, q % 3, :], st[:, 1, q % 2, :], act_g[:, q % 2, :],
                                          ALU.mult).then_inc(s_hd, 1)
                    if q == 4 and not first:
                        add_output(c - 1)
                    if q == 5:
                        route_scores(sc)
                    elif q == 7:
                        route_largest()
                    elif q == 9:
                        route_groups()
                    elif q == 11:
                        route_experts()
                    elif q == 13:
                        route_weights()
                    elif q == 15:
                        keep_weights(c + 1)
                per_chunk[0] = steps[0] - start

            per_chunk = [0]
            chunks(dve, body)
            add_output(NCH - 1)


_INS = ['x', 'ctx_768', 'L0_xattn_Wq', 'L0_xattn_Wk', 'L0_xattn_Wv', 'L0_xattn_Wo', 'L0_xattn_bo',
        'L0_ffn_router_weight', 'L0_ffn_router_bias', 'L0_ffn_gate_w', 'L0_ffn_up_w', 'L0_ffn_down_w',
        'L0_ffn_shared_gate_w', 'L0_ffn_shared_up_w', 'L0_ffn_shared_down_w']


def kernel(**inputs):
    import numpy as np
    import concourse.bacc as bacc
    from concourse.bass_utils import run_bass_kernel_spmd

    nc = bacc.Bacc("TRN2", target_bir_lowering=False, num_devices=1)
    arrays, args = {}, []
    for name in _INS:
        a = np.ascontiguousarray(inputs[name])
        arrays[f"in_{name}"] = a
        args.append(nc.dram_tensor(f"in_{name}", a.shape, mybir.dt.from_np(a.dtype), kind="ExternalInput").ap())
    out = nc.dram_tensor("out_x", inputs["x"].shape, F32, kind="ExternalOutput").ap()
    xattn_moe(nc, *args, out)
    r = run_bass_kernel_spmd(nc, [arrays], core_ids=[0])
    return r.results[0]["out_x"]
```
